# Optimizing a Trainium2 kernel written in Bass

```python
import numpy as np
import jax
import jax.numpy as jnp

def _softmax(x, axis=-1):
    return jax.nn.softmax(x, axis=axis)

def _gelu(x):
    return jax.nn.gelu(x, approximate=True)

def _silu(x):
    return jax.nn.silu(x)

def _sigmoid(x):
    return jax.nn.sigmoid(x)

def _layernorm(x, axis=-1, eps=1e-05):
    m = jnp.mean(x, axis=axis, keepdims=True)
    v = jnp.var(x, axis=axis, keepdims=True)
    return (x - m) / jnp.sqrt(v + eps)

def _scatter_add(tgt, idx, src, axis=0):
    return tgt.at[idx].add(src)

def _segment_sum(src, seg, n):
    return jax.ops.segment_sum(src, seg, n)
kernel_name = 'mk_adaln_ffn_d1_seqx_r2_412dc3'

def setup_inputs(seed: int=0):
    np.random.seed(seed)
    _w = jnp.asarray

    def _rec_inputs():
        import jax
        import jax.numpy as jnp
        _rk = jax.random.key(seed)
        x = -0.0003929 + 0.9999 * jax.random.normal(jax.random.fold_in(_rk, 1), (32, 128, 512), jnp.float32)
        _lenS = 128 - jax.random.randint(jax.random.fold_in(_rk, 7), (32,), 0, max(1, 128 // 4) + 1, jnp.int32)
        _lenS2 = 128 - jax.random.randint(jax.random.fold_in(_rk, 8), (32,), 0, max(1, 128 // 4) + 1, jnp.int32)
        itok_B_0_63 = jax.random.randint(jax.random.fold_in(_rk, 11), (32,), 0, 64, jnp.int32)
        return (x, itok_B_0_63)
    x, itok_B_0_63 = _rec_inputs()

    def _L0_cond_setup():
        import jax, jax.numpy as jnp
        import numpy as np
        NUM_CATEGORIES = 64
        INPUT_DIM = 512
        HIDDEN_DIM = 512
        B = 128
        S = 64
        key = jax.random.key(seed)
        kx, kc, kw = jax.random.split(key, 3)
        x = jax.random.normal(kx, (B, S, INPUT_DIM), dtype=jnp.float32)
        cat_ids = jax.random.randint(kc, (B,), 0, NUM_CATEGORIES, dtype=jnp.int32)
        W = 0.02 * jax.random.normal(kw, (NUM_CATEGORIES, INPUT_DIM, HIDDEN_DIM), dtype=jnp.float32)
        b = jnp.zeros((NUM_CATEGORIES, HIDDEN_DIM), dtype=jnp.float32)
        return {'x': x, 'cat_ids': cat_ids, 'W': W, 'b': b}
    _L0_cond_all = _L0_cond_setup()
    _L0_cond_in = {k: v for k, v in _L0_cond_all.items() if k in ('W', 'b')}
    del _L0_cond_all

    def _L0_ffn_setup():
        import jax, jax.numpy as jnp
        import numpy as np
        BLOCK = 32
        W_BITS = 4
        ACT_BITS = 16

        def act_qdq(x):
            qmax = 2.0 ** (ACT_BITS - 1) - 1.0
            scale = jnp.maximum(jnp.max(jnp.abs(x)) / qmax, 1e-12)
            return jnp.clip(jnp.round(x / scale), -qmax - 1.0, qmax) * scale

        def fixed_qdq_u16(x):
            scale = 1.0 / 65536.0
            return jnp.clip(jnp.round(x / scale), 0.0, 65535.0) * scale

        def lpbq_dequant(w):
            O, I = w.shape
            qmax = 2.0 ** (W_BITS - 1) - 1.0
            wb = w.reshape(O, I // BLOCK, BLOCK)
            s = jnp.maximum(jnp.max(jnp.abs(wb), axis=-1, keepdims=True) / qmax, 1e-12)
            wq = jnp.clip(jnp.round(wb / s), -qmax - 1.0, qmax) * s
            return wq.reshape(O, I)
        key = jax.random.key(seed)
        k1, k2, k3, k4 = jax.random.split(key, 4)
        B, S, H, I = (2, 2048, 512, 1536)
        x = jax.random.normal(k1, (B, S, H), jnp.float32)
        w_gate = jax.random.normal(k2, (I, H), jnp.float32) * 0.02
        w_up = jax.random.normal(k3, (I, H), jnp.float32) * 0.02
        w_down = jax.random.normal(k4, (H, I), jnp.float32) * 0.02
        return {'x': x, 'w_gate': w_gate, 'w_up': w_up, 'w_down': w_down}
    _L0_ffn_all = _L0_ffn_setup()
    _L0_ffn_in = {k: v for k, v in _L0_ffn_all.items() if k in ('w_gate', 'w_up', 'w_down')}
    del _L0_ffn_all
    return {'x': x, 'itok_B_0_63': itok_B_0_63, 'L0_cond_W': _L0_cond_in['W'], 'L0_cond_b': _L0_cond_in['b'], 'L0_ffn_w_gate': _L0_ffn_in['w_gate'], 'L0_ffn_w_up': _L0_ffn_in['w_up'], 'L0_ffn_w_down': _L0_ffn_in['w_down']}

def reference(x, itok_B_0_63, L0_cond_W, L0_cond_b, L0_ffn_w_gate, L0_ffn_w_up, L0_ffn_w_down):
    import jax
    import jax.numpy as jnp

    def _L0_cond_ref(x, cat_ids, W, b):
        import jax, jax.numpy as jnp
        import numpy as np
        NUM_CATEGORIES = 64
        INPUT_DIM = 512
        HIDDEN_DIM = 512
        B = 128
        S = 64
        selected_W = W[cat_ids]
        selected_b = b[cat_ids]
        out = jnp.einsum('bsd,bdh->bsh', x, selected_W) + selected_b[:, None, :]
        return out

    def _L0_ffn_ref(x, w_gate, w_up, w_down):
        import jax, jax.numpy as jnp
        import numpy as np
        BLOCK = 32
        W_BITS = 4
        ACT_BITS = 16

        def act_qdq(x):
            qmax = 2.0 ** (ACT_BITS - 1) - 1.0
            scale = jnp.maximum(jnp.max(jnp.abs(x)) / qmax, 1e-12)
            return jnp.clip(jnp.round(x / scale), -qmax - 1.0, qmax) * scale

        def fixed_qdq_u16(x):
            scale = 1.0 / 65536.0
            return jnp.clip(jnp.round(x / scale), 0.0, 65535.0) * scale

        def lpbq_dequant(w):
            O, I = w.shape
            qmax = 2.0 ** (W_BITS - 1) - 1.0
            wb = w.reshape(O, I // BLOCK, BLOCK)
            s = jnp.maximum(jnp.max(jnp.abs(wb), axis=-1, keepdims=True) / qmax, 1e-12)
            wq = jnp.clip(jnp.round(wb / s), -qmax - 1.0, qmax) * s
            return wq.reshape(O, I)
        x = act_qdq(x)
        up = act_qdq(x @ lpbq_dequant(w_up).T)
        gate = act_qdq(x @ lpbq_dequant(w_gate).T)
        sig = fixed_qdq_u16(jax.nn.sigmoid(gate))
        gate = act_qdq(gate * sig)
        o = act_qdq(gate * up)
        return o @ lpbq_dequant(w_down).T
    x = x + _L0_ffn_ref(_L0_cond_ref(x, itok_B_0_63, L0_cond_W, L0_cond_b), L0_ffn_w_gate, L0_ffn_w_up, L0_ffn_w_down)
    return x

_drawn_inputs = setup_inputs


def setup_inputs(seed=0):
    import zlib

    import numpy as np

    out = dict(_drawn_inputs(seed))
    spreads = {'L0_cond_b': (0.0, 0.8)}
    factors = {'L0_cond_W': 3.134, 'L0_ffn_w_gate': 3.112, 'L0_ffn_w_up': 3.134, 'L0_ffn_w_down': 3.098}
    for name, (base, spread) in spreads.items():
        noise = np.random.default_rng([zlib.crc32(name.encode()), seed]).standard_normal(out[name].shape)
        drawn = base * np.exp(spread * noise) if base else spread * noise
        out[name] = jnp.asarray(drawn.astype(out[name].dtype))
    for name, factor in factors.items():
        out[name] = (out[name] * factor).astype(out[name].dtype)
    return out
```

```python
from contextlib import ExitStack

import concourse.bass as bass
from concourse import mybir

B, S, H = 32, 128, 512
CATS = 64
INNER = 1536
BLOCK = 32

P = 128
CHUNK = 512
CHUNKS = B * S // CHUNK
BPC = CHUNK // S
KH = H // P
NT = INNER // P
ROW = NT * CHUNK
PIECE_TILES = 3
PIECE = PIECE_TILES * CHUNK
Q = NT // PIECE_TILES
PIECES = Q * CHUNKS
WCOLS = INNER * H // P
WBLOCKS = WCOLS // BLOCK
TILE_BLOCKS = 512 // BLOCK
SLICES = 3
WSLICES = WCOLS // 512
BANKS = 6

ACT_QMAX = 32767.0
W_QMAX = 7.0
TINY = 1e-12
ROUND = 1.5 * 2.0 ** 23
ROUND32 = ROUND * 32
RMAX = bass.bass_isa.ReduceOp.max


def adaln_ffn(nc, x, cats, cond_w, cond_b, w_gate, w_up, w_down, out):
    f32, f16, i16 = mybir.dt.float32, mybir.dt.float16, mybir.dt.int16
    i32, u16, bf16 = mybir.dt.int32, mybir.dt.uint16, mybir.dt.bfloat16
    ALU, ACT, AX = mybir.AluOpType, mybir.ActivationFunctionType, mybir.AxisListType

    gate_dram = nc.dram_tensor("gate_scratch", (CHUNKS, P, ROW), f32, kind="Internal").ap()
    up_dram = nc.dram_tensor("up_scratch", (CHUNKS, P, ROW), f32, kind="Internal").ap()
    gcode_dram = nc.dram_tensor("gate_code_scratch", (CHUNKS, P, ROW), i16, kind="Internal").ap()
    act_dram = nc.dram_tensor("act_code_scratch", (CHUNKS, P, ROW), i16, kind="Internal").ap()

    ctx = ExitStack()
    with ctx:
        arena = ctx.enter_context(nc.sbuf_tensor("arena", [P, 206 * 1024], mybir.dt.uint8))
        base = nc.sbuf_base - 206 * 1024

        def place(name, offset, shape, dt):
            return nc.alloc_sbuf_tensor_at(name, [P] + shape, dt, offset=base + offset)

        K = 1024
        cond = place("cond", 0, [CHUNKS, KH, CHUNK], f32)
        xq = place("xq", 0, [CHUNKS, 2, KH, CHUNK], f16)
        wt_gate = place("wt_gate", 64 * K, [2, KH, INNER], f16)
        wt_up = place("wt_up", 88 * K, [2, KH, INNER], f16)
        wt_down = place("wt_down", 112 * K, [2, NT, H], f16)
        w_ring = place("w_ring", 88 * K, [BPC, KH, H], f32)
        x_ring = place("x_ring", 120 * K, [BPC, H], f32)
        xt = place("xt", 128 * K, [2, KH, S], f32)
        R = 136 * K
        wf = place("wf", R, [WSLICES, 512], f32)
        ws = place("ws", R + 24 * K, [SLICES, 512], f32)
        wparts = place("wparts", R + 30 * K, [SLICES, 2, 512], f16)
        wd_tile = place("wd_tile", R + 36 * K, [INNER], f32)
        xcode = place("xcode", R + 42 * K, [KH * CHUNK], i16)
        bias_rows = place("bias_rows", R + 36 * K, [H], f32)
        onehot = place("onehot", R + 38 * K, [B], f32)
        stage = place("stage", R + 46 * K, [2, PIECE_TILES, CHUNK], f32)
        big_in = place("big_in", 64 * K, [Q, PIECE], f32)
        code_ring = place("code_ring", R, [Q, PIECE], i16)
        sig = place("sig", R + 12 * K, [2, PIECE], f32)
        sigq = place("sigq", R + 24 * K, [2, PIECE], u16)
        mag = place("mag", R + 30 * K, [2, PIECE], i16)
        junk = place("junk", R + 36 * K, [PIECE], bf16)
        neg = place("neg", R + 39 * K, [PIECE], i16)
        o_parts = place("o_parts", 0, [2, 2, NT, CHUNK], f16)
        ucode = place("ucode", 48 * K, [Q, PIECE], i16)
        ocode = place("ocode", R + 12 * K, [2, PIECE], i16)
        x_res = place("x_res", 88 * K, [BPC, H], f32)
        y_out = place("y_out", 96 * K, [BPC, H], f32)
        C = R + 58 * K
        wstep = place("wstep", C, [3, WBLOCKS], f32)
        wrecip = place("wrecip", C + 2304, [3, WBLOCKS], f32)
        ident32 = place("ident32", C + 4608, [P], f32)
        ident16 = place("ident16", C + 5120, [P], f16)
        bias = place("bias", C + 5376, [B, KH], f32)
        cat_f = place("cat_f", C + 5888, [B], f32)
        cat_row = place("cat_row", C + 6016, [B], i32)
        part_i = place("part_i", C + 6144, [1], i32)
        part_f = place("part_f", C + 6176, [1], f32)
        cond_max = place("cond_max", C + 6208, [CHUNKS], f32)
        tile_max = place("tile_max", C + 6240, [2 * PIECES], f32)
        p_max = place("p_max", C + 6496, [2, 2 * Q], f32)
        o_max = place("o_max", C + 6624, [2, Q], f32)
        NS = 48
        scal = place("scal", C + 6752, [NS], f32)
        cat_id = place("cat_id", C + 6976, [B], i32)
        assert C + 7104 <= 206 * K
        names = iter(range(NS))

        def scalar_column():
            n = next(names)
            return scal[:, n:n + 1]

        psum = [ctx.enter_context(nc.psum_tensor(f"bank{n}", [P, CHUNK], f32)) for n in range(6)]
        wt_bank = ctx.enter_context(nc.psum_tensor("wt_bank", [P, 2, KH, P], f16))
        bias_bank = ctx.enter_context(nc.psum_tensor("bias_bank", [P, 512], f32))

        def sem(name):
            return ctx.enter_context(nc.semaphore(name))

        idx_in, bias_in, wgate_in, wup_in = sem("idx_in"), sem("bias_in"), sem("wgate_in"), sem("wup_in")
        w_in = [sem(f"w_in{n}") for n in range(BPC)]
        x_in = [sem(f"x_in{n}") for n in range(BPC)]
        consts, idents = sem("consts"), sem("idents")
        onehot_made, bias_summed, bias_ready = sem("onehot_made"), sem("bias_summed"), sem("bias_ready")
        x_turned, x_copied = sem("x_turned"), sem("x_copied")
        cond_done, cond_copied = sem("cond_done"), sem("cond_copied")
        w_scaled, w_rounded, w_stepped = sem("w_scaled"), sem("w_rounded"), sem("w_stepped")
        w_high, w_low, w_turned, wt_ready = sem("w_high"), sem("w_low"), sem("w_turned"), sem("wt_ready")
        wscale_ready = sem("wscale_ready")
        wdown_tile_in, wdown_maxed = sem("wdown_tile_in"), sem("wdown_maxed")
        wdown_in = [sem(f"wdown_in{m}") for m in range(KH)]
        xcode_made, xhigh_made, xq_ready = sem("xcode_made"), sem("xhigh_made"), sem("xq_ready")
        tile_done, tile_copied, piece_maxed = sem("tile_done"), sem("tile_copied"), sem("piece_maxed")
        stage_out = [sem(f"stage_out{n}") for n in range(2)]
        gate_in = [sem(f"gate_in{n}") for n in range(Q)]
        gcode_out = [sem(f"gcode_out{n}") for n in range(Q)]
        gcode_in = [sem(f"gcode_in{n}") for n in range(Q)]
        act_out = [sem(f"act_out{n}") for n in range(Q)]
        code_made, sig_made, sigq_pool, sigq_made = sem("code_made"), sem("sig_made"), sem("sigq_pool"), sem("sigq_made")
        neg_made, mag_made, mag_act, step_done = sem("neg_made"), sem("mag_made"), sem("mag_act"), sem("step_done")
        up_in = [sem(f"up_in{n}") for n in range(Q)]
        act_in = [sem(f"act_in{n}") for n in range(Q)]
        ucode_made, prod_used = sem("ucode_made"), sem("prod_used")
        ocode_made, ohigh_made, o_ready = sem("ocode_made"), sem("ohigh_made"), sem("o_ready")
        xres_in = [sem(f"xres_in{n}") for n in range(BPC)]
        y_out_done = [sem(f"y_out_done{n}") for n in range(BPC)]
        out_done, y_made = sem("out_done"), sem("y_made")
        p_merged, o_merged = sem("p_merged"), sem("o_merged")
        part_max, all_max = sem("part_max"), sem("all_max")
        scalar_step, scale_ready = sem("scalar_step"), sem("scale_ready")

        pm = [scalar_column() for _ in range(8)]
        am = [scalar_column() for _ in range(8)]
        (WG, WU, COND, WD, GATE, ACTV, UP, PROD) = range(8)
        w_mul = [scalar_column() for _ in range(3)]
        w_div = [scalar_column() for _ in range(3)]
        s_x, k_x = scalar_column(), scalar_column()
        s_g, k_g, s_u, k_u = (scalar_column() for _ in range(4))
        c_p, s_p, k_p = (scalar_column() for _ in range(3))
        c_o, s_o, k_o, k_y = (scalar_column() for _ in range(4))
        tmp = [scalar_column() for _ in range(3)]
        R_X, R_GATE, R_ACT, R_UP, R_PROD = 1, 2, 3, 4, 5

        x_flat = x
        wg_view = w_gate.rearrange("(n p) h -> p n h", p=P)
        wu_view = w_up.rearrange("(n p) h -> p n h", p=P)
        wd_view = w_down.rearrange("(m p) i -> p m i", p=P)
        wf_down = wf[:, :, :].rearrange("p (m j) c -> p m (j c)", m=KH)

        def chunk_rows(dram, i, q):
            return dram[bass.ds(i, 1), :, q * PIECE:(q + 1) * PIECE].rearrange("a p n -> (a p) n")

        def held(eng, value):
            if not isinstance(value, int):
                eng.compute_val(value)
            return value

        block = ctx.enter_context(nc.Block())

        @block.sync
        def _(sp):
            def load_batch(i, r, first):
                b = BPC * i + r
                cat = sp.value_load(cat_id[0:1, bass.ds(b, 1)], min_val=0, max_val=CATS - 1)
                sp.wait_ge(idx_in, 16)
                if not first:
                    sp.wait_ge(x_turned, b - BPC + 1)
                sp.dma_start(x_ring[:, r, :],
                             x_flat[bass.ds(b, 1), :, :].rearrange("a s d -> (a s) d")).then_inc(x_in[r], 16)
                sp.wait_ge(idx_in, 16)
                if not first:
                    sp.wait_ge(cond_done, b - BPC + 1)
                sp.dma_start(w_ring[:, r, :, :],
                             cond_w[bass.ds(cat, 1), :, :].rearrange("a (k p) h -> p (a k) h", p=P))\
                    .then_inc(w_in[r], 16)

            sp.dma_start(cat_id[0:1, :], cats.rearrange("(a n) -> a n", a=1)).then_inc(idx_in, 16)
            sp.wait_ge(idx_in, 16)
            for r in range(BPC):
                load_batch(0, r, True)
            with sp.Fori(1, CHUNKS) as i:
                for r in range(BPC):
                    load_batch(i, r, False)

            with sp.Fori(0, KH) as m:
                sp.wait_ge(idx_in, 16)
                sp.wait_ge(wdown_maxed, m + 1)
                sp.dma_start(wd_tile[:, :], wd_view[:, bass.ds(m, 1), :].rearrange("p a i -> p (a i)"))\
                    .then_inc(wdown_tile_in, 16)
            sp.wait_ge(w_stepped, 2 * WSLICES)
            for m in range(KH):
                sp.dma_start(wf_down[:, m, :], wd_view[:, m, :]).then_inc(wdown_in[m], 16)

            def load_gate(i, u):
                sp.dma_start(big_in[:, u % Q, :], chunk_rows(gate_dram, 2 * i + u // Q, u % Q))\
                    .then_inc(gate_in[u % Q], 16)

            def gate_codes(i, last):
                for u in range(2 * Q):
                    made = held(sp, 2 * Q * i + u + 1)
                    sp.wait_ge(idx_in, 16)
                    sp.wait_ge(code_made, made)
                    sp.dma_start(chunk_rows(gcode_dram, 2 * i + u // Q, u % Q), code_ring[:, u % Q, :])\
                        .then_inc(gcode_out[u % Q], 16)
                    if u < Q:
                        load_gate(i, u + Q)
                    elif not last:
                        load_gate(i + 1, u - Q)

            sp.wait_ge(stage_out[0], 16 * PIECES // 2)
            sp.wait_ge(stage_out[1], 16 * PIECES // 2)
            sp.wait_ge(tile_done, NT * CHUNKS)
            for u in range(Q):
                load_gate(0, u)
            with sp.Fori(0, 3) as i:
                gate_codes(i, False)
            gate_codes(3, True)

            def load_codes(i, u):
                sp.dma_start(code_ring[:, u % Q, :], chunk_rows(gcode_dram, 2 * (i - 4) + u // Q, u % Q))\
                    .then_inc(gcode_in[u % Q], 16)

            def act_codes(i, first, last):
                for u in range(2 * Q):
                    made = held(sp, 2 * Q * i + u + 1)
                    sp.wait_ge(idx_in, 16)
                    sp.wait_ge(step_done, made)
                    sp.dma_start(chunk_rows(act_dram, 2 * (i - 4) + u // Q, u % Q), code_ring[:, u % Q, :])\
                        .then_inc(act_out[u % Q], 16)
                    if first and u < 2:
                        load_codes(i, u + 2)
                    elif u < 2 * Q - 2:
                        stored = held(sp, 32 * (i - 4) + 16 * ((u + 2) // Q))
                        sp.wait_ge(idx_in, 16)
                        sp.wait_ge(act_out[(u - 2) % Q], stored)
                        load_codes(i, u + 2)
                    elif not last:
                        stored = held(sp, 32 * (i - 4) + 32)
                        sp.wait_ge(idx_in, 16)
                        sp.wait_ge(act_out[(u - 2) % Q], stored)
                        load_codes(i + 1, u + 2 - 2 * Q)

            sp.wait_ge(step_done, 2 * PIECES // 2)
            for n in range(Q):
                sp.wait_ge(gcode_out[n], 16 * PIECES // Q)
            load_codes(4, 0)
            load_codes(4, 1)
            act_codes(4, True, False)
            with sp.Fori(5, 7) as i:
                act_codes(i, False, False)
            act_codes(7, False, True)

            def load_pair(i, q):
                sp.dma_start(big_in[:, q, :], chunk_rows(up_dram, i, q)).then_inc(up_in[q], 16)
                sp.dma_start(code_ring[:, q, :], chunk_rows(act_dram, i, q)).then_inc(act_in[q], 16)

            for n in range(2):
                sp.wait_ge(stage_out[n], 16 * PIECES)
            for n in range(Q):
                sp.wait_ge(act_out[n], 16 * PIECES // Q)
            for q in range(Q):
                load_pair(0, q)
            with sp.Fori(1, CHUNKS) as i:
                for q in range(Q):
                    sp.wait_ge(idx_in, 16)
                    sp.wait_ge(prod_used, Q * i + q - Q + 1)
                    load_pair(i, q)
            for q in range(Q):
                sp.wait_ge(prod_used, PIECES + q - Q + 1)
                load_pair(0, q)
            for r in range(BPC):
                sp.dma_start(x_res[:, r, :], x_flat[r, :, :]).then_inc(xres_in[r], 16)
            for q in range(Q):
                sp.wait_ge(prod_used, PIECES + q + 1)
                load_pair(1, q)

            def stores(i, more_x, more_pairs):
                for r in range(BPC):
                    sp.wait_ge(idx_in, 16)
                    sp.wait_ge(y_made, BPC * i + r + 1)
                    sp.dma_start(out[bass.ds(BPC * i + r, 1), :, :].rearrange("a s h -> (a s) h"), y_out[:, r, :])\
                        .then_inc(y_out_done[r], 16)
                    if more_x:
                        sp.dma_start(x_res[:, r, :],
                                     x_flat[bass.ds(BPC * i + BPC + r, 1), :, :].rearrange("a s d -> (a s) d"))\
                            .then_inc(xres_in[r], 16)
                    if more_pairs:
                        sp.wait_ge(idx_in, 16)
                        sp.wait_ge(prod_used, PIECES + Q * i + Q + r + 1)
                        load_pair(i + 2, r)

            with sp.Fori(0, CHUNKS - 2) as i:
                stores(i, True, True)
            stores(CHUNKS - 2, True, False)
            stores(CHUNKS - 1, False, False)
            for r in range(BPC):
                sp.wait_ge(y_out_done[r], 16 * CHUNKS)

        @block.gpsimd
        def _(pool):
            nc.gpsimd.iota(part_i[:, :], pattern=[[0, 1]], base=0, channel_multiplier=1).then_inc(consts, 1)
            nc.gpsimd.memset(ident32[:, :], 0.0).then_inc(idents, 1)
            nc.gpsimd.memset(ident16[:, :], 0.0).then_inc(idents, 1)
            pool.wait_ge(idents, 2)
            for ident in (ident32, ident16):
                nc.gpsimd.affine_select(out=ident[:, :], in_=ident[:, :], compare_op=ALU.not_equal, fill=1.0,
                                        base=0, pattern=[[-1, P]], channel_multiplier=1).then_inc(idents, 1)

            def over_partitions(which):
                pool.wait_ge(part_max, which + 1)
                nc.gpsimd.partition_all_reduce(am[which], pm[which], P, RMAX).then_inc(all_max, 1)

            for which in (WG, WU, COND, WD, GATE):
                over_partitions(which)

            def codes(i, first):
                for u in range(2 * Q):
                    loaded = held(pool, 32 * i + (16 if u < Q else 32))
                    stored = held(pool, 32 * i + (0 if u < Q else 16))
                    read = held(pool, 2 * Q * i + u - Q + 1)
                    pool.wait_ge(scale_ready, R_GATE)
                    pool.wait_ge(gate_in[u % Q], loaded)
                    if not first or u >= Q:
                        pool.wait_ge(gcode_out[u % Q], stored)
                        pool.wait_ge(step_done, read)
                    nc.gpsimd.tensor_scalar(code_ring[:, u % Q, :], big_in[:, u % Q, :], k_g, 0.0,
                                            ALU.mult, ALU.add).then_inc(code_made, 1)
                    if u % 2 == 1:
                        if u >= 3:
                            sigmoid_code(i, u - 2, first)
                        elif not first:
                            sigmoid_code(i - 1, 2 * Q - 1, False)

            def sigmoid_code(i, u, first):
                made, used = held(pool, 2 * Q * i + u + 1), held(pool, 2 * Q * i + u - 1)
                pool.wait_ge(scale_ready, R_GATE)
                pool.wait_ge(sig_made, made)
                if not (first and u == 1):
                    pool.wait_ge(step_done, used)
                nc.gpsimd.tensor_scalar(sigq[:, 1, :], sig[:, 1, :], 65536.0, 65535.0,
                                        ALU.mult, ALU.min).then_inc(sigq_pool, 1)

            pool.wait_ge(scale_ready, R_GATE)
            codes(0, True)
            with pool.Fori(1, 4) as i:
                codes(i, False)
            sigmoid_code(3, 2 * Q - 1, False)

            for which in (ACTV, UP, PROD):
                over_partitions(which)

        @block.scalar
        def _(act):
            act.dma_start(cat_row[0:CATS, :], cats.rearrange("(a n) -> a n", a=1).to_broadcast([CATS, B]))\
                .then_inc(bias_in, 16)
            act.dma_start(bias_rows[0:CATS, :], cond_b).then_inc(bias_in, 16)
            act.dma_start(wf[:, :, :], wg_view).then_inc(wgate_in, 16)

            def copy_xt(i, r, first):
                b = BPC * i + r
                act.wait_ge(x_turned, b + 1)
                if not first or r >= 2:
                    act.wait_ge(cond_done, b - 1)
                nc.scalar.activation(xt[:, r % 2, :, :], psum[4 + r % 2][:, :].rearrange("p (k s) -> p k s", k=KH),
                                     ACT.Copy).then_inc(x_copied, 1)

            def high_part(w, it, j, first):
                n = WSLICES * w + SLICES * it + j
                act.wait_ge(w_stepped, n + 1)
                if not first:
                    act.wait_ge(w_turned, n - SLICES + 1)
                nc.scalar.activation(wparts[:, j, 0, :], ws[:, j, :], ACT.Copy, scale=w_mul[w])\
                    .then_inc(w_high, 1)

            def copy_wt(w, it, j):
                n = WSLICES * w + SLICES * it + j
                act.wait_ge(w_turned, n + 1)
                if w < 2:
                    dst = (wt_gate, wt_up)[w][:, :, :, bass.ds((SLICES * it + j) * P, P)]
                else:
                    dst = wt_down[:, :, 4 * j:4 * j + 4, bass.ds(it * P, P)]
                nc.scalar.activation(dst, wt_bank[:, :, :, :], ACT.Copy).then_inc(wt_ready, 1)

            def cond_chunk(i, first, weights):
                for r in range(BPC):
                    copy_xt(i, r, first)
                    if weights and r < SLICES:
                        if first and r == 0:
                            act.wait_ge(wscale_ready, 1)
                        high_part(0, i, r, first)
                    if weights and r >= 2:
                        copy_wt(0, i, r - 2)
                if weights:
                    copy_wt(0, i, SLICES - 1)

            cond_chunk(0, True, True)
            with act.Fori(1, 4) as i:
                cond_chunk(i, False, True)
            act.wait_ge(w_stepped, WSLICES)
            act.dma_start(wf[:, :, :], wu_view).then_inc(wup_in, 16)
            with act.Fori(4, CHUNKS) as i:
                cond_chunk(i, False, False)

            def copy_tile(i, n, first, dram, side):
                q, t = n // PIECE_TILES, NT * i + n
                done = 16 * (Q // 2) * i + 16 * (q // 2)
                if n % PIECE_TILES == 0 and (not first or q >= 2):
                    act.wait_ge(stage_out[q % 2], done)
                    act.wait_ge(piece_maxed, Q * i + q - 1)
                act.wait_ge(tile_done, t + 1)
                nc.scalar.activation(stage[:, q % 2, n % PIECE_TILES, :], psum[n % BANKS][:, :], ACT.Copy)\
                    .then_inc(tile_copied, 1)
                if n % PIECE_TILES == PIECE_TILES - 1:
                    act.wait_ge(tile_copied, t + 1)
                    act.dma_start(chunk_rows(dram, i - side * CHUNKS, q),
                                  stage[:, q % 2, :, :].rearrange("p t c -> p (t c)")).then_inc(stage_out[q % 2], 16)

            def gate_chunk(i, first, w):
                it = i if w == 1 else i - 4
                for n in range(NT):
                    copy_tile(i, n, first, gate_dram, 0)
                    if n % 4 == 1:
                        high_part(w, it, n // 4, False)
                    if n % 4 == 3:
                        copy_wt(w, it, n // 4)

            act.wait_ge(wscale_ready, 2)
            gate_chunk(0, True, 1)
            with act.Fori(1, 4) as i:
                gate_chunk(i, False, 1)
            act.wait_ge(wscale_ready, 3)
            with act.Fori(4, CHUNKS) as i:
                gate_chunk(i, False, 2)

            def sigmoid(i, u, first, second_half):
                n = 2 * Q * i + u
                if second_half:
                    act.wait_ge(gcode_in[u % Q], 32 * (i - 4) + (16 if u < Q else 32))
                else:
                    act.wait_ge(code_made, n + 1)
                if not first or u >= 2:
                    act.wait_ge(step_done, n - 1)
                nc.scalar.activation(sig[:, u % 2, :], code_ring[:, u % Q, :], ACT.Sigmoid, scale=s_g)\
                    .then_inc(sig_made, 1)
                if not second_half and u % 2 == 1:
                    nc.scalar.activation(mag[:, 1, :], code_ring[:, u % Q, :], ACT.Abs).then_inc(mag_act, 1)

            def up_chunk(i, first, second_half):
                u = 0
                for n in range(NT):
                    copy_tile(CHUNKS + i, n, False, up_dram, 1)
                    if n % 3 != 1:
                        if first and u == 0:
                            act.wait_ge(scale_ready, R_GATE)
                        sigmoid(i, u, first, second_half)
                        u += 1

            up_chunk(0, True, False)
            with act.Fori(1, 4) as i:
                up_chunk(i, False, False)
            with act.Fori(4, CHUNKS) as i:
                up_chunk(i, False, True)

            def up_magnitudes(i, first):
                for q in range(Q):
                    act.wait_ge(up_in[q], 16 * i + 16)
                    if not first:
                        act.wait_ge(prod_used, Q * i + q - Q + 1)
                    nc.scalar.activation(ucode[:, q, :], big_in[:, q, :], ACT.Abs, scale=k_u)\
                        .then_inc(ucode_made, 1)
                    if q % 2 == 1:
                        act.wait_ge(act_in[q], 16 * i + 16)
                        if not first or q >= 2:
                            act.wait_ge(prod_used, Q * i + q - 1)
                        nc.scalar.activation(mag[:, 1, :], code_ring[:, q, :], ACT.Abs).then_inc(mag_act, 1)

            def up_codes(i):
                for q in range(Q):
                    act.wait_ge(up_in[q], 16 * i + 16)
                    act.wait_ge(prod_used, Q * i + q - Q + 1)
                    nc.scalar.activation(ucode[:, q, :], big_in[:, q, :], ACT.Copy, scale=k_u)\
                        .then_inc(ucode_made, 1)

            act.wait_ge(scale_ready, R_UP)
            up_magnitudes(0, True)
            with act.Fori(1, CHUNKS) as i:
                up_magnitudes(i, False)
            with act.Fori(CHUNKS, 2 * CHUNKS) as i:
                up_codes(i)

        @block.tensor
        def _(pe):
            pe.wait_ge(idents, 4)

            def turn_x(i, r, first):
                b = BPC * i + r
                pe.wait_ge(x_in[r], 16 * i + 16)
                if not first or r >= 2:
                    pe.wait_ge(x_copied, b - 1)
                for k in range(KH):
                    mm = nc.tensor.transpose(psum[4 + r % 2][:, k * S:(k + 1) * S],
                                             x_ring[:, r, k * P:(k + 1) * P], ident32[:, :])
                mm.then_inc(x_turned, 1)

            def cond_matmul(i, r, first):
                b = BPC * i + r
                pe.wait_ge(x_copied, b + 1)
                pe.wait_ge(w_in[r], 16 * i + 16)
                if not first:
                    pe.wait_ge(cond_copied, b - BPC + 1)
                for m in range(KH):
                    for k in range(KH):
                        mm = nc.tensor.matmul(psum[r][:, m * S:(m + 1) * S], w_ring[:, r, k, m * P:(m + 1) * P],
                                              xt[:, r % 2, k, :], start=(k == 0), stop=(k == KH - 1))
                mm.then_inc(cond_done, 1)

            def turn_w(w, it, j, first):
                n = WSLICES * w + SLICES * it + j
                pe.wait_ge(w_low, n + 1)
                if not first:
                    pe.wait_ge(wt_ready, n)
                for h in range(2):
                    for k in range(4):
                        mm = nc.tensor.transpose(wt_bank[:, h, k, :], wparts[:, j, h, k * P:(k + 1) * P], ident16[:, :])
                mm.then_inc(w_turned, 1)

            def cond_chunk(i, first, last, weights):
                for r in range(BPC):
                    if r < BPC - 1:
                        turn_x(i, r + 1, first)
                    elif not last:
                        turn_x(i + 1, 0, False)
                    cond_matmul(i, r, first)
                    if weights and r >= 1:
                        turn_w(0, i, r - 1, first and r == 1)

            turn_x(0, 0, True)
            pe.wait_ge(onehot_made, 1)
            for m in range(KH):
                mm = nc.tensor.matmul(bias_bank[:, m * B:(m + 1) * B], bias_rows[0:CATS, m * P:(m + 1) * P],
                                      onehot[0:CATS, :], start=True, stop=True)
            mm.then_inc(bias_summed, 1)
            cond_chunk(0, True, False, True)
            with pe.Fori(1, 4) as i:
                cond_chunk(i, False, False, True)
            with pe.Fori(4, CHUNKS - 1) as i:
                cond_chunk(i, False, False, False)
            cond_chunk(CHUNKS - 1, False, True, False)

            def tile_matmul(i, c, n, wt, first):
                t = NT * i + n
                if not first or n >= BANKS:
                    pe.wait_ge(tile_copied, t - BANKS + 1)
                bank = psum[n % BANKS]
                for k in range(KH):
                    w_hi, w_lo = (wt[:, h, k, n * P:(n + 1) * P] for h in range(2))
                    x_hi, x_lo = (xq[:, bass.ds(c, 1), h, k, :].rearrange("p a s -> p (a s)") for h in range(2))
                    nc.tensor.matmul(bank[:, :], w_hi, x_hi, start=(k == 0), stop=False)
                    nc.tensor.matmul(bank[:, :], w_hi, x_lo, start=False, stop=False)
                    mm = nc.tensor.matmul(bank[:, :], w_lo, x_hi, start=False, stop=(k == KH - 1))
                mm.then_inc(tile_done, 1)

            def gate_chunk(i, first, w):
                it = i if w == 1 else i - 4
                pe.wait_ge(xq_ready, i + 1)
                for n in range(NT):
                    tile_matmul(i, i, n, wt_gate, first)
                    if n % 4 == 3:
                        turn_w(w, it, n // 4, False)

            pe.wait_ge(wt_ready, WSLICES)
            gate_chunk(0, True, 1)
            with pe.Fori(1, 4) as i:
                gate_chunk(i, False, 1)
            with pe.Fori(4, CHUNKS) as i:
                gate_chunk(i, False, 2)
            with pe.Fori(CHUNKS, 2 * CHUNKS) as i:
                for n in range(NT):
                    tile_matmul(i, i - CHUNKS, n, wt_up, False)

            def down_chunk(i, h, first):
                for r in range(BPC):
                    if not first:
                        pe.wait_ge(y_made, BPC * i + r - BPC + 1)
                    for k in range(NT):
                        if r == 0 and k % PIECE_TILES == 0:
                            pe.wait_ge(o_ready, Q * i + k // PIECE_TILES + 1)
                        o_hi, o_lo = (o_parts[:, h, part, k, r * P:(r + 1) * P] for part in range(2))
                        nc.tensor.matmul(psum[r][:, :], o_hi, wt_down[:, 0, k, :], start=(k == 0), stop=False)
                        nc.tensor.matmul(psum[r][:, :], o_hi, wt_down[:, 1, k, :], start=False, stop=False)
                        mm = nc.tensor.matmul(psum[r][:, :], o_lo, wt_down[:, 0, k, :], start=False, stop=(k == NT - 1))
                    mm.then_inc(out_done, 1)

            pe.wait_ge(tile_copied, 2 * NT * CHUNKS)
            down_chunk(0, 0, True)
            down_chunk(1, 1, False)
            with pe.Fori(1, CHUNKS // 2) as pair:
                for h in range(2):
                    down_chunk(2 * pair + h, h, False)

        @block.vector
        def _(dve):
            steps = [0]

            def link(ins):
                steps[0] += 1
                ins.then_inc(scalar_step, 1)
                dve.wait_ge(scalar_step, steps[0])

            V = nc.vector

            dve.wait_ge(consts, 1)
            link(V.tensor_copy(part_f[:, :], part_i[:, :]))
            dve.wait_ge(bias_in, 32)
            link(V.tensor_copy(cat_f[0:CATS, :], cat_row[0:CATS, :]))
            V.tensor_scalar(onehot[0:CATS, :], cat_f[0:CATS, :], part_f[0:CATS, 0:1], None,
                            ALU.is_equal).then_inc(onehot_made, 1)

            def weight_steps(w, which):
                link(V.tensor_scalar(wstep[:, w, :], wstep[:, w, :], 1.0 / W_QMAX, TINY, ALU.mult, ALU.max))
                link(V.reciprocal(wrecip[:, w, :], wstep[:, w, :]))
                V.tensor_reduce(pm[which], wstep[:, w, :], AX.X, ALU.max).then_inc(part_max, 1)

            def weight_scale(w, which):
                dve.wait_ge(all_max, which + 1)
                mul_i, div_i, e_i = (a.bitcast(i32) for a in (w_mul[w], w_div[w], tmp[1]))
                link(V.tensor_scalar(tmp[0], am[which], W_QMAX, None, ALU.mult))
                link(V.tensor_scalar(e_i, tmp[0].bitcast(i32), 23, None, ALU.logical_shift_right))
                link(V.tensor_scalar(tmp[2].bitcast(i32), e_i, -1.0, 268.0, ALU.mult, ALU.add))
                link(V.tensor_scalar(mul_i, tmp[2].bitcast(i32), 23, None, ALU.logical_shift_left))
                link(V.tensor_scalar(tmp[2].bitcast(i32), e_i, 14.0, None, ALU.subtract))
                steps[0] += 1
                V.tensor_scalar(div_i, tmp[2].bitcast(i32), 23, None, ALU.logical_shift_left).then_inc(scalar_step, 1)
                dve.wait_ge(scalar_step, steps[0])
                V.tensor_copy(tmp[0], am[which]).then_inc(wscale_ready, 1)

            def blocks(a, w, it, j):
                at = (SLICES * it + j) * TILE_BLOCKS
                return a[:, w, bass.ds(at, TILE_BLOCKS)].unsqueeze(2).to_broadcast([P, TILE_BLOCKS, BLOCK])

            def quantise_slice(w, it, j):
                n = WSLICES * w + SLICES * it + j
                src = wf[:, bass.ds(SLICES * it + j, 1), :].rearrange("p a (g e) -> p (a g) e", e=BLOCK)
                dst = ws[:, j, :].rearrange("p (g e) -> p g e", e=BLOCK)
                V.tensor_tensor(dst, src, blocks(wrecip, w, it, j), ALU.mult).then_inc(w_scaled, 1)
                dve.wait_ge(w_scaled, n + 1)
                V.tensor_scalar(ws[:, j, :], ws[:, j, :], ROUND, ROUND, ALU.add, ALU.subtract).then_inc(w_rounded, 1)
                dve.wait_ge(w_rounded, n + 1)
                V.tensor_tensor(dst, dst, blocks(wstep, w, it, j), ALU.mult).then_inc(w_stepped, 1)

            def low_part(w, it, j):
                n = WSLICES * w + SLICES * it + j
                dve.wait_ge(w_high, n + 1)
                V.scalar_tensor_tensor(out=wparts[:, j, 1, :], in0=ws[:, j, :], scalar=w_mul[w], in1=wparts[:, j, 0, :],
                                       op0=ALU.mult, op1=ALU.subtract).then_inc(w_low, 1)

            def add_bias(i, r):
                b = BPC * i + r
                dve.wait_ge(cond_done, b + 1)
                V.tensor_tensor(cond[:, bass.ds(i, 1), :, r * S:(r + 1) * S].rearrange("p a k s -> p (a k) s"),
                                psum[r][:, :].rearrange("p (k s) -> p k s", k=KH),
                                bias[:, bass.ds(b, 1), :].rearrange("p a k -> p (a k)").unsqueeze(2).to_broadcast([P, KH, S]),
                                ALU.add).then_inc(cond_copied, 1)

            def cond_chunk(i, weights):
                for r in range(BPC):
                    if weights and r < SLICES:
                        quantise_slice(0, i, r)
                    if weights and r >= 1:
                        low_part(0, i, r - 1)
                    add_bias(i, r)
                dve.wait_ge(cond_copied, BPC * i + BPC)
                V.tensor_reduce(cond_max[:, bass.ds(i, 1)],
                                cond[:, bass.ds(i, 1), :, :].rearrange("p a k s -> p (a k s)"),
                                AX.X, ALU.max, apply_absolute_value=True)

            dve.wait_ge(wgate_in, 16)
            link(V.tensor_reduce(wstep[:, 0, :], wf[:, :, :].rearrange("p n (g e) -> p (n g) e", e=BLOCK),
                                 AX.X, ALU.max, apply_absolute_value=True))
            weight_steps(0, WG)
            weight_scale(0, WG)
            dve.wait_ge(bias_summed, 1)
            link(V.tensor_copy(bias[:, :, :], bias_bank[:, 0:KH * B].rearrange("p (k b) -> p b k", k=KH)))
            cond_chunk(0, True)
            with dve.Fori(1, 4) as i:
                cond_chunk(i, True)
            with dve.Fori(4, CHUNKS - 1) as i:
                cond_chunk(i, False)
            dve.wait_ge(wup_in, 16)
            link(V.tensor_reduce(wstep[:, 1, :], wf[:, :, :].rearrange("p n (g e) -> p (n g) e", e=BLOCK),
                                 AX.X, ALU.max, apply_absolute_value=True))
            weight_steps(1, WU)
            for r in range(BPC):
                add_bias(CHUNKS - 1, r)
            dve.wait_ge(cond_copied, B)
            link(V.tensor_reduce(cond_max[:, CHUNKS - 1:CHUNKS], cond[:, CHUNKS - 1, :, :].rearrange("p k s -> p (k s)"),
                                 AX.X, ALU.max, apply_absolute_value=True))
            V.tensor_reduce(pm[COND], cond_max[:, :], AX.X, ALU.max).then_inc(part_max, 1)
            weight_scale(1, WU)

            dve.wait_ge(all_max, COND + 1)
            link(V.tensor_scalar(s_x, am[COND], 1.0 / ACT_QMAX, TINY, ALU.mult, ALU.max))
            link(V.reciprocal(k_x, s_x))

            def x_codes(i):
                whole = cond[:, bass.ds(i, 1), :, :].rearrange("p a k s -> p (a k s)")
                high, low = (xq[:, bass.ds(i, 1), h, :, :].rearrange("p a k s -> p (a k s)") for h in range(2))
                V.tensor_scalar(xcode[:, :], whole, k_x, None, ALU.mult).then_inc(xcode_made, 1)
                dve.wait_ge(xcode_made, i + 1)
                V.tensor_scalar(high, xcode[:, :], ROUND32, ROUND32, ALU.add, ALU.subtract).then_inc(xhigh_made, 1)
                dve.wait_ge(xhigh_made, i + 1)
                V.tensor_tensor(low, xcode[:, :], high, ALU.subtract).then_inc(xq_ready, 1)
                dve.wait_ge(xq_ready, i + 1)

            def piece_max(i, q):
                dve.wait_ge(tile_copied, NT * i + PIECE_TILES * (q + 1))
                V.tensor_reduce(tile_max[:, bass.ds(Q * i + q, 1)], stage[:, q % 2, :, :].rearrange("p t c -> p (t c)"),
                                AX.X, ALU.max, apply_absolute_value=True).then_inc(piece_maxed, 1)

            def gate_chunk(i, w, last):
                it = i if w == 1 else i - 4
                if not last:
                    x_codes(i + 1)
                for q in range(Q):
                    if q < SLICES:
                        if w == 2 and q == 0:
                            dve.wait_ge(wdown_in[KH - 1], 16)
                        quantise_slice(w, it, q)
                        low_part(w, it, q)
                    piece_max(i, q)
                if w == 1:
                    dve.wait_ge(wdown_tile_in, 16 * i + 16)
                    V.tensor_reduce(wstep[:, 2, bass.ds(i * (WBLOCKS // KH), WBLOCKS // KH)],
                                    wd_tile[:, :].rearrange("p (g e) -> p g e", e=BLOCK),
                                    AX.X, ALU.max, apply_absolute_value=True).then_inc(wdown_maxed, 1)

            x_codes(0)
            V.tensor_copy(tmp[0], s_x).then_inc(wdown_maxed, 1)
            gate_chunk(0, 1, False)
            with dve.Fori(1, 4) as i:
                gate_chunk(i, 1, False)
            dve.wait_ge(wdown_maxed, KH + 1)
            weight_steps(2, WD)
            weight_scale(2, WD)
            for m in range(KH):
                dve.wait_ge(wdown_in[m], 16)
            with dve.Fori(4, CHUNKS - 1) as i:
                gate_chunk(i, 2, False)
            gate_chunk(CHUNKS - 1, 2, True)

            def step_from_max(which, values, unit, step, factor):
                V.tensor_reduce(pm[which], values, AX.X, ALU.max).then_inc(part_max, 1)
                dve.wait_ge(all_max, which + 1)
                link(V.tensor_scalar(tmp[0], am[which], unit, 1.0 / ACT_QMAX, ALU.mult, ALU.mult))
                link(V.tensor_scalar(step, tmp[0], TINY, None, ALU.max))
                link(V.reciprocal(tmp[1], step))
                V.tensor_scalar(factor, tmp[1], unit, None, ALU.mult).then_inc(scale_ready, 1)

            dve.wait_ge(piece_maxed, PIECES)
            link(V.tensor_scalar(tmp[2], s_x, w_div[0], None, ALU.mult))
            steps[0] += 1
            V.tensor_copy(tmp[0], tmp[2]).then_inc(scalar_step, 1)
            dve.wait_ge(scalar_step, steps[0])
            V.tensor_copy(tmp[1], s_x).then_inc(scale_ready, 1)
            step_from_max(GATE, tile_max[:, 0:PIECES], tmp[2], s_g, k_g)

            def magnitude(src, count):
                V.tensor_scalar(neg[:, :], src, -1.0, None, ALU.mult).then_inc(neg_made, 1)
                dve.wait_ge(neg_made, count + 1)
                V.tensor_tensor(mag[:, 0, :], src, neg[:, :], ALU.max).then_inc(mag_made, 1)

            def max_step(i, u):
                n, pair = held(dve, 2 * Q * i + u), held(dve, Q * i + u // 2 + 1)
                if u % 2 == 0:
                    dve.wait_ge(code_made, n + 1)
                    magnitude(code_ring[:, u % Q, :], Q * i + u // 2)
                    dve.wait_ge(sig_made, n + 1)
                    V.tensor_scalar(sigq[:, 0, :], sig[:, 0, :], 65536.0, 65535.0, ALU.mult, ALU.min)\
                        .then_inc(sigq_made, 1)
                dve.wait_ge(scale_ready, R_GATE)
                if u % 2 == 0:
                    dve.wait_ge(mag_made, pair)
                    dve.wait_ge(sigq_made, pair)
                else:
                    dve.wait_ge(mag_act, pair)
                    dve.wait_ge(sigq_pool, pair)
                if not (isinstance(i, int) and u == 0):
                    dve.wait_ge(step_done, n)
                V.tensor_tensor_reduce(junk[:, :], mag[:, u % 2, :], sigq[:, u % 2, :], 1.0, 0.0, ALU.mult, ALU.max,
                                       p_max[:, 0, u:u + 1]).then_inc(step_done, 1)

            def act_step(i, u):
                n = 2 * Q * i + u
                dve.wait_ge(sig_made, n + 1)
                V.tensor_scalar(sigq[:, u % 2, :], sig[:, u % 2, :], 65536.0, 65535.0, ALU.mult, ALU.min)\
                    .then_inc(sigq_made, 1)
                dve.wait_ge(sigq_made, Q * 4 + 2 * Q * (i - 4) + u + 1)
                V.scalar_tensor_tensor(out=code_ring[:, u % Q, :], in0=code_ring[:, u % Q, :], scalar=k_p,
                                       in1=sigq[:, u % 2, :], op0=ALU.mult, op1=ALU.mult).then_inc(step_done, 1)

            def up_chunk(i, step):
                for q in range(Q):
                    step(i, 2 * q)
                    step(i, 2 * q + 1)
                    piece_max(CHUNKS + i, q)

            link(V.memset(p_max[:, 1, :], 0.0))

            def up_chunk_max(i):
                up_chunk(i, max_step)
                dve.wait_ge(step_done, 2 * Q * i + 2 * Q)
                V.tensor_tensor(p_max[:, 1, :], p_max[:, 1, :], p_max[:, 0, :], ALU.max).then_inc(p_merged, 1)
                dve.wait_ge(p_merged, i + 1)

            up_chunk_max(0)
            with dve.Fori(1, 4) as i:
                up_chunk_max(i)
            link(V.tensor_scalar(c_p, s_g, 1.0 / 65536.0, None, ALU.mult))
            step_from_max(ACTV, p_max[:, 1, :], c_p, s_p, k_p)
            dve.wait_ge(scale_ready, R_ACT)
            with dve.Fori(4, CHUNKS) as i:
                up_chunk(i, act_step)
            dve.wait_ge(piece_maxed, 2 * PIECES)
            link(V.tensor_scalar(tmp[2], s_x, w_div[1], None, ALU.mult))
            step_from_max(UP, tile_max[:, PIECES:2 * PIECES], tmp[2], s_u, k_u)

            def product_max(i, q):
                n, pair = held(dve, Q * i + q), held(dve, PIECES // 2 + Q // 2 * i + q // 2 + 1)
                made = held(dve, Q * i + q + 1)
                if q % 2 == 0:
                    dve.wait_ge(act_in[q], 16 * i + 16)
                    magnitude(code_ring[:, q, :], PIECES // 2 + Q // 2 * i + q // 2)
                dve.wait_ge(scale_ready, R_UP)
                dve.wait_ge(mag_act if q % 2 else mag_made, pair)
                dve.wait_ge(ucode_made, made)
                if not (isinstance(i, int) and q == 0):
                    dve.wait_ge(prod_used, n)
                V.tensor_tensor_reduce(junk[:, :], mag[:, q % 2, :], ucode[:, q, :], 1.0, 0.0, ALU.mult, ALU.max,
                                       o_max[:, 0, q:q + 1]).then_inc(prod_used, 1)

            link(V.memset(o_max[:, 1, :], 0.0))

            def product_chunk_max(i):
                for q in range(Q):
                    product_max(i, q)
                dve.wait_ge(prod_used, Q * i + Q)
                V.tensor_tensor(o_max[:, 1, :], o_max[:, 1, :], o_max[:, 0, :], ALU.max).then_inc(o_merged, 1)
                dve.wait_ge(o_merged, i + 1)

            product_chunk_max(0)
            with dve.Fori(1, CHUNKS) as i:
                product_chunk_max(i)
            link(V.tensor_scalar(c_o, s_p, s_u, None, ALU.mult))
            step_from_max(PROD, o_max[:, 1, :], c_o, s_o, k_o)
            dve.wait_ge(scale_ready, R_PROD)
            link(V.tensor_scalar(k_y, s_o, w_div[2], None, ALU.mult))

            def product_codes(i, q, h, first):
                n = Q * i + q
                high, low = (o_parts[:, h, part, PIECE_TILES * q:PIECE_TILES * (q + 1), :]
                             .rearrange("p t c -> p (t c)") for part in range(2))
                dve.wait_ge(act_in[q], 16 * (CHUNKS + i) + 16)
                dve.wait_ge(ucode_made, PIECES + n + 1)
                V.scalar_tensor_tensor(out=ocode[:, q % 2, :], in0=code_ring[:, q, :], scalar=k_o, in1=ucode[:, q, :],
                                       op0=ALU.mult, op1=ALU.mult).then_inc(prod_used, 1)
                dve.wait_ge(prod_used, PIECES + n + 1)
                if not first and q == 0:
                    dve.wait_ge(out_done, BPC * (i - 1))
                V.tensor_scalar(high, ocode[:, q % 2, :], ROUND32, ROUND32, ALU.add, ALU.subtract)\
                    .then_inc(ohigh_made, 1)
                dve.wait_ge(ohigh_made, n + 1)
                V.tensor_tensor(low, ocode[:, q % 2, :], high, ALU.subtract).then_inc(o_ready, 1)

            def finish_tile(i, r, first):
                dve.wait_ge(out_done, BPC * i + r + 1)
                dve.wait_ge(xres_in[r], 16 * i + 16)
                if not first:
                    dve.wait_ge(y_out_done[r], 16 * i)
                V.scalar_tensor_tensor(out=y_out[:, r, :], in0=psum[r][:, :], scalar=k_y, in1=x_res[:, r, :],
                                       op0=ALU.mult, op1=ALU.add).then_inc(y_made, 1)

            for q in range(Q):
                product_codes(0, q, 0, True)
            for q in range(Q):
                product_codes(1, q, 1, True)
                finish_tile(0, q, True)
            with dve.Fori(1, CHUNKS // 2) as pair:
                for h in range(2):
                    i = 2 * pair + h
                    for q in range(Q):
                        product_codes(i, q, h, False)
                        finish_tile(i - 1, q, False)
            for r in range(BPC):
                finish_tile(CHUNKS - 1, r, False)


_INS = ['x', 'itok_B_0_63', 'L0_cond_W', 'L0_cond_b', 'L0_ffn_w_gate', 'L0_ffn_w_up', 'L0_ffn_w_down']
_OUTS = [((B, S, H), 'float32')]


def kernel(**inputs):
    import numpy as _np
    import concourse.bacc as _bacc
    from concourse import mybir as _mybir
    from concourse.bass_utils import run_bass_kernel_spmd as _run

    nc = _bacc.Bacc("TRN2", target_bir_lowering=False, num_devices=1)
    arrays, args = {}, []
    for name in _INS:
        a = _np.ascontiguousarray(inputs[name])
        arrays[f"in_{name}_dram"] = a
        args.append(nc.dram_tensor(f"in_{name}_dram", a.shape, _mybir.dt.from_np(a.dtype), kind="ExternalInput").ap())
    for i, (shape, dtype) in enumerate(_OUTS):
        dt = _mybir.dt.from_np(_np.dtype(dtype))
        args.append(nc.dram_tensor(f"out_{i}_dram", shape, dt, kind="ExternalOutput").ap())
    adaln_ffn(nc, *args)
    r = _run(nc, [arrays], core_ids=[0])
    got = tuple(r.results[0][f"out_{i}_dram"] for i in range(len(_OUTS)))
    return got[0]
```

```python
from contextlib import ExitStack

import concourse.bass as bass
from concourse import mybir

B, S, H = 32, 128, 512
CATS = 64
INNER = 1536
BLOCK = 32

P = 128
CHUNK = 512
CHUNKS = B * S // CHUNK
BPC = CHUNK // S
KH = H // P
NT = INNER // P
ROW = NT * CHUNK
PIECE_TILES = 3
PIECE = PIECE_TILES * CHUNK
Q = NT // PIECE_TILES
PIECES = Q * CHUNKS
WCOLS = INNER * H // P
WBLOCKS = WCOLS // BLOCK
TILE_BLOCKS = 512 // BLOCK
SLICES = 3
WSLICES = WCOLS // 512
BANKS = 6
FIRST_STEPS, LOOP_STEPS = 8, 6
HALF = 5
ACT_STEPS = (11, 11, 10)
GSLOTS = 3
CSLOTS = 4
POOL_FIRST, POOL_LOOP = 5, 3
USLOTS = 6
MAG_SLOT = {1: 1, 3: 1, 4: 2, 5: 1}

ACT_QMAX = 32767.0
W_QMAX = 7.0
TINY = 1e-12
ROUND = 1.5 * 2.0 ** 23
ROUND32 = ROUND * 32
RMAX = bass.bass_isa.ReduceOp.max


def adaln_ffn(nc, x, cats, cond_w, cond_b, w_gate, w_up, w_down, out):
    f32, f16, i16 = mybir.dt.float32, mybir.dt.float16, mybir.dt.int16
    i32, u16, bf16 = mybir.dt.int32, mybir.dt.uint16, mybir.dt.bfloat16
    ALU, ACT, AX = mybir.AluOpType, mybir.ActivationFunctionType, mybir.AxisListType

    gate_dram = nc.dram_tensor("gate_scratch", (PIECES, P, PIECE), f32, kind="Internal").ap()
    up_dram = nc.dram_tensor("up_scratch", (PIECES, P, PIECE), f32, kind="Internal").ap()
    gcode_dram = nc.dram_tensor("gate_code_scratch", (PIECES, P, PIECE), i16, kind="Internal").ap()

    ctx = ExitStack()
    with ctx:
        arena = ctx.enter_context(nc.sbuf_tensor("arena", [P, 207 * 1024], mybir.dt.uint8))
        base = nc.sbuf_base - 207 * 1024

        def place(name, offset, shape, dt):
            return nc.alloc_sbuf_tensor_at(name, [P] + shape, dt, offset=base + offset)

        K = 1024
        wt_gate = place("wt_gate", 0, [2, KH, INNER], f16)
        gate_ring = place("gate_ring", 0, [GSLOTS, PIECE], f32)
        cond_head = place("cond_head", 24 * K, [CHUNKS - 1, KH, CHUNK], f32)
        xq_head = place("xq_head", 24 * K, [CHUNKS - 1, 2, KH, CHUNK], f16)
        bias_rows = place("bias_rows", 80 * K, [H], f32)
        onehot = place("onehot", 82 * K, [B], f32)
        xcode = place("xcode", 84 * K, [KH * CHUNK], i16)
        wd_tile = place("wd_tile", 88 * K, [INNER], f32)
        mag = place("mag", 80 * K, [2, PIECE], i16)
        junk = place("junk", 86 * K, [PIECE], bf16)
        act_codes = place("act_codes", 0, [PIECES, PIECE], i16)
        wt_up = place("wt_up", 96 * K, [2, KH, INNER], f16)
        wt_down = place("wt_down", 120 * K, [2, NT, H], f16)
        w_ring = place("w_ring", 96 * K, [BPC, KH, H], f32)
        x_ring = place("x_ring", 128 * K, [BPC, H], f32)
        xt = place("xt", 136 * K, [2, KH, S], f32)
        R = 144 * K
        wf = place("wf", R, [WSLICES, 512], f32)
        ws = place("ws", R + 24 * K, [SLICES, 512], f32)
        wparts = place("wparts", R + 30 * K, [SLICES, 2, 512], f16)
        stage = place("stage", R + 36 * K, [2, PIECE_TILES, CHUNK], f32)
        code_ring = place("code_ring", R, [CSLOTS, PIECE], i16)
        sig = place("sig", R + 12 * K, [2, PIECE], f32)
        sigq = place("sigq", R + 24 * K, [2, PIECE], u16)
        sig_int = place("sig_int", R + 12 * K, [2, PIECE], i32)
        pcode = place("pcode", R + 24 * K, [2, PIECE], f32)
        cond_last = place("cond_last", R + 48 * K, [1, KH, CHUNK], f32)
        xq_last = place("xq_last", R + 48 * K, [1, 2, KH, CHUNK], f16)
        up_head = place("up_head", 96 * K, [USLOTS - 2, PIECE], f32)
        up_tail = place("up_tail", R + 36 * K, [2, PIECE], f32)
        umag = place("umag", R, [2, PIECE], i16)
        pmag = place("pmag", R + 6 * K, [3, PIECE], i16)
        pjunk = place("pjunk", R + 15 * K, [2, PIECE], bf16)
        pneg = place("pneg", R + 21 * K, [PIECE], i16)
        o_parts = [place("o_parts0", 96 * K, [2, NT, CHUNK], f16), place("o_parts1", R, [2, NT, CHUNK], f16)]
        up_again = place("up_again", R + 24 * K, [2, PIECE], f32)
        ucode = place("ucode", R + 36 * K, [2, PIECE], i16)
        ocode = place("ocode", R + 42 * K, [2, PIECE], i16)
        x_res = place("x_res", R + 48 * K, [2, H], f32)
        y_out = place("y_out", R + 52 * K, [2, H], f32)
        C = R + 56 * K
        wstep = place("wstep", C, [3, WBLOCKS], f32)
        wrecip = place("wrecip", C + 2304, [3, WBLOCKS], f32)
        ident32 = place("ident32", C + 4608, [P], f32)
        ident16 = place("ident16", C + 5120, [P], f16)
        bias = place("bias", C + 5376, [B, KH], f32)
        cat_f = place("cat_f", C + 5888, [B], f32)
        cat_row = place("cat_row", C + 6016, [B], i32)
        part_i = place("part_i", C + 6144, [1], i32)
        part_f = place("part_f", C + 6176, [1], f32)
        cond_max = place("cond_max", C + 6208, [CHUNKS + 1], f32)
        tile_max = place("tile_max", C + 6272, [2, PIECES + 1], f32)
        p_max = place("p_max", C + 6560, [2, FIRST_STEPS], f32)
        o_max = place("o_max", C + 6624, [2, USLOTS], f32)
        NS = 48
        scal = place("scal", C + 6688, [NS], f32)
        cat_id = place("cat_id", C + 6880, [B], i32)
        assert C + 7008 <= 207 * K

        def cond_chunk_at(i):
            last = isinstance(i, int) and i == CHUNKS - 1
            return cond_last[:, 0:1, :, :] if last else cond_head[:, bass.ds(i, 1), :, :]

        def xq_at(i, part):
            last = isinstance(i, int) and i == CHUNKS - 1
            return xq_last[:, 0:1, part, :, :] if last else xq_head[:, bass.ds(i, 1), part, :, :]

        def act_piece(n):
            return act_codes[:, bass.ds(n, 1), :].rearrange("p a n -> p (a n)")

        def up_slot(s):
            return up_head[:, s, :] if s < USLOTS - 2 else up_tail[:, s - USLOTS + 2, :]

        def gate_step(i, u):
            if isinstance(i, int) and i == 0:
                return u, u % GSLOTS, u // GSLOTS
            lead = FIRST_STEPS - LOOP_STEPS
            return LOOP_STEPS * i + lead + u, (lead + u) % GSLOTS, LOOP_STEPS // GSLOTS * i + (lead + u) // GSLOTS

        def pool_step(i):
            return POOL_FIRST if isinstance(i, int) and i == 0 else POOL_LOOP

        def steps_of(i):
            return FIRST_STEPS if isinstance(i, int) and i == 0 else LOOP_STEPS

        names = iter(range(NS))

        def scalar_column():
            n = next(names)
            return scal[:, n:n + 1]

        psum = [ctx.enter_context(nc.psum_tensor(f"bank{n}", [P, CHUNK], f32)) for n in range(6)]
        wt_bank = ctx.enter_context(nc.psum_tensor("wt_bank", [P, 2, KH, P], f16))
        bias_bank = ctx.enter_context(nc.psum_tensor("bias_bank", [P, 512], f32))

        def sem(name):
            return ctx.enter_context(nc.semaphore(name))

        idx_in, bias_in, wgate_in, wup_in = sem("idx_in"), sem("bias_in"), sem("wgate_in"), sem("wup_in")
        w_in = [sem(f"w_in{n}") for n in range(BPC)]
        x_in = [sem(f"x_in{n}") for n in range(BPC)]
        consts, idents = sem("consts"), sem("idents")
        onehot_made, bias_summed, bias_ready = sem("onehot_made"), sem("bias_summed"), sem("bias_ready")
        x_turned, x_copied = sem("x_turned"), sem("x_copied")
        cond_done, cond_copied = sem("cond_done"), sem("cond_copied")
        w_scaled, w_rounded, w_stepped = sem("w_scaled"), sem("w_rounded"), sem("w_stepped")
        w_high, w_low, w_turned, wt_ready = sem("w_high"), sem("w_low"), sem("w_turned"), sem("wt_ready")
        wscale_ready = sem("wscale_ready")
        wblocks_maxed = sem("wblocks_maxed")
        wdown_tile_in, wdown_maxed = sem("wdown_tile_in"), sem("wdown_maxed")
        wdown_in = [sem(f"wdown_in{m}") for m in range(KH)]
        xcode_made, xhigh_made, xq_ready = sem("xcode_made"), sem("xhigh_made"), sem("xq_ready")
        tile_done, tile_copied, piece_maxed = sem("tile_done"), sem("tile_copied"), sem("piece_maxed")
        part_maxed = sem("part_maxed")
        stage_out = [sem(f"stage_out{n}") for n in range(2)]
        gate_in = [sem(f"gate_in{n}") for n in range(GSLOTS)]
        gcode_out = [sem(f"gcode_out{n}") for n in range(GSLOTS)]
        gcode_in = [sem(f"gcode_in{n}") for n in range(CSLOTS)]
        code_made, sig_made, sigq_pool, sigq_made = sem("code_made"), sem("sig_made"), sem("sigq_pool"), sem("sigq_made")
        neg_made, mag_made, step_done = sem("neg_made"), sem("mag_made"), sem("step_done")
        sig_scaled, pcode_pool, pcode_act = sem("sig_scaled"), sem("pcode_pool"), sem("pcode_act")
        up_in = [sem(f"up_in{n}") for n in range(USLOTS)]
        umag_made, pmag_made, pmag_act, max_used = sem("umag_made"), sem("pmag_made"), sem("pmag_act"), sem("max_used")
        up_again_in = [sem(f"up_again_in{n}") for n in range(2)]
        ucode_made, prod_used = sem("ucode_made"), sem("prod_used")
        ocode_made, ohigh_made, o_ready = sem("ocode_made"), sem("ohigh_made"), sem("o_ready")
        xres_in = [sem(f"xres_in{n}") for n in range(2)]
        y_out_done = [sem(f"y_out_done{n}") for n in range(2)]
        out_done, y_made = sem("out_done"), sem("y_made")
        p_merged, o_merged = sem("p_merged"), sem("o_merged")
        part_max, all_max = sem("part_max"), sem("all_max")
        scalar_step, scale_ready = sem("scalar_step"), sem("scale_ready")

        pm = [scalar_column() for _ in range(8)]
        am = [scalar_column() for _ in range(8)]
        (WG, COND, WU, WD, GATE, ACTV, UP, PROD) = range(8)
        w_mul = [scalar_column() for _ in range(3)]
        w_div = [scalar_column() for _ in range(3)]
        s_x, k_x = scalar_column(), scalar_column()
        s_g, k_g, s_u, k_u = (scalar_column() for _ in range(4))
        c_p, s_p, k_p = (scalar_column() for _ in range(3))
        c_o, s_o, k_o, k_y = (scalar_column() for _ in range(4))
        tmp = [scalar_column() for _ in range(3)]
        R_X, R_GATE, R_ACT, R_UP, R_PROD = 1, 2, 3, 4, 5

        x_flat = x
        wg_view = w_gate.rearrange("(n p) h -> p n h", p=P)
        wu_view = w_up.rearrange("(n p) h -> p n h", p=P)
        wd_view = w_down.rearrange("(m p) i -> p m i", p=P)
        wf_down = wf[:, :, :].rearrange("p (m j) c -> p m (j c)", m=KH)

        def piece_rows(dram, n):
            return dram[bass.ds(n, 1), :, :].rearrange("a p n -> (a p) n")

        def held(eng, value):
            if not isinstance(value, int):
                eng.compute_val(value)
            return value

        block = ctx.enter_context(nc.Block())

        @block.sync
        def _(sp):
            def load_x_batch(i, r, first):
                b = BPC * i + r
                if not first:
                    turned = held(sp, b - BPC + 1)
                    sp.wait_ge(idx_in, 16)
                    sp.wait_ge(x_turned, turned)
                sp.dma_start(x_ring[:, r, :],
                             x_flat[bass.ds(b, 1), :, :].rearrange("a s d -> (a s) d")).then_inc(x_in[r], 16)

            def load_w_batch(i, r, first):
                b = BPC * i + r
                cat = sp.value_load(cat_id[0:1, bass.ds(b, 1)], min_val=0, max_val=CATS - 1)
                sp.wait_ge(idx_in, 16)
                if not first:
                    sp.wait_ge(cond_done, b - BPC + 1)
                sp.dma_start(w_ring[:, r, :, :],
                             cond_w[bass.ds(cat, 1), :, :].rearrange("a (k p) h -> p (a k) h", p=P))\
                    .then_inc(w_in[r], 16)

            sp.dma_start(cat_id[0:1, :], cats.rearrange("(a n) -> a n", a=1)).then_inc(idx_in, 16)
            load_x_batch(0, 0, True)
            sp.wait_ge(idx_in, 16)
            for r in range(BPC):
                load_w_batch(0, r, True)
                if r < BPC - 1:
                    load_x_batch(0, r + 1, True)

            def load_chunk(i, gate_part):
                for r in range(BPC):
                    load_x_batch(i, r, False)
                    load_w_batch(i, r, False)
                    if gate_part is not None and r % 2 == 1:
                        at = SLICES * (gate_part + r // 2)
                        sp.dma_start(wf[:, at:at + SLICES, :], wg_view[:, at:at + SLICES, :]).then_inc(wgate_in, 16)

            load_chunk(1, 0)
            load_chunk(2, 2)
            with sp.Fori(3, CHUNKS) as i:
                load_chunk(i, None)
            sp.wait_ge(w_stepped, WSLICES)
            sp.dma_start(wf[:, :, :], wu_view).then_inc(wup_in, 16)

            with sp.Fori(0, KH) as m:
                sp.wait_ge(idx_in, 16)
                sp.wait_ge(wdown_maxed, m + 1)
                sp.dma_start(wd_tile[:, :], wd_view[:, bass.ds(m, 1), :].rearrange("p a i -> p (a i)"))\
                    .then_inc(wdown_tile_in, 16)
            sp.wait_ge(w_stepped, 2 * WSLICES)
            for m in range(KH):
                sp.dma_start(wf_down[:, m, :], wd_view[:, m, :]).then_inc(wdown_in[m], 16)

            def load_gate(n, s):
                sp.dma_start(gate_ring[:, s, :], piece_rows(gate_dram, n)).then_inc(gate_in[s], 16)

            def gate_codes(i, last):
                for u in range(steps_of(i)):
                    n, s, _ = gate_step(i, u)
                    made = held(sp, n + 1)
                    sp.wait_ge(idx_in, 16)
                    sp.wait_ge(code_made, made)
                    sp.dma_start(piece_rows(gcode_dram, n), code_ring[:, s, :]).then_inc(gcode_out[s], 16)
                    if not last or u < LOOP_STEPS - GSLOTS:
                        load_gate(n + GSLOTS, s)

            sp.wait_ge(stage_out[0], 16 * PIECES // 2)
            sp.wait_ge(stage_out[1], 16 * PIECES // 2)
            sp.wait_ge(tile_done, NT * CHUNKS)
            for s in range(GSLOTS):
                load_gate(s, s)
            gate_codes(0, False)
            with sp.Fori(1, HALF - 1) as i:
                gate_codes(i, False)
            gate_codes(HALF - 1, True)

            def load_codes(n, s):
                sp.dma_start(code_ring[:, s, :], piece_rows(gcode_dram, n)).then_inc(gcode_in[s], 16)

            sp.wait_ge(step_done, PIECES)
            for s in range(GSLOTS):
                sp.wait_ge(gcode_out[s], 16 * ((PIECES - s + GSLOTS - 1) // GSLOTS))
            for s in range(CSLOTS):
                load_codes(s, s)
            with sp.Fori(1, PIECES // CSLOTS) as turn:
                for s in range(CSLOTS):
                    used = held(sp, PIECES + CSLOTS * turn + s - CSLOTS + 1)
                    sp.wait_ge(idx_in, 16)
                    sp.wait_ge(step_done, used)
                    load_codes(CSLOTS * turn + s, s)

            def load_up(n, s):
                sp.dma_start(up_slot(s), piece_rows(up_dram, n)).then_inc(up_in[s], 16)

            for n in range(2):
                sp.wait_ge(stage_out[n], 16 * (PIECES - 1))
            sp.wait_ge(tile_done, 2 * NT * CHUNKS)
            for s in range(USLOTS - 2):
                load_up(s, s)
            for n in range(2):
                sp.wait_ge(stage_out[n], 16 * PIECES)
            for s in range(USLOTS - 2, USLOTS):
                sp.wait_ge(umag_made, s - USLOTS + 3)
                load_up(s, s)
            with sp.Fori(1, (PIECES - 2) // USLOTS) as turn:
                for s in range(USLOTS):
                    used = held(sp, 2 + USLOTS * turn + s - USLOTS + 1)
                    sp.wait_ge(idx_in, 16)
                    sp.wait_ge(umag_made, used)
                    load_up(USLOTS * turn + s, s)

            def load_again(n, q):
                sp.dma_start(up_again[:, q % 2, :], piece_rows(up_dram, n)).then_inc(up_again_in[q % 2], 16)

            def load_x(b, r):
                sp.dma_start(x_res[:, r % 2, :], x_flat[bass.ds(b, 1), :, :].rearrange("a s d -> (a s) d"))\
                    .then_inc(xres_in[r % 2], 16)

            sp.wait_ge(step_done, 2 * PIECES)
            for q in range(2):
                load_again(q, q)
                load_x(q, q)
            for q in range(Q):
                sp.wait_ge(prod_used, q + 1)
                load_again(q + 2, q)

            def finish_chunk(i, pairs_left, last):
                for r in range(BPC):
                    if r < pairs_left:
                        used = held(sp, Q * i + Q + r + 1)
                        sp.wait_ge(idx_in, 16)
                        sp.wait_ge(prod_used, used)
                        load_again(Q * i + Q + r + 2, r)
                    made = held(sp, BPC * i + r + 1)
                    sp.wait_ge(idx_in, 16)
                    sp.wait_ge(y_made, made)
                    sp.dma_start(out[bass.ds(BPC * i + r, 1), :, :].rearrange("a s h -> (a s) h"),
                                 y_out[:, r % 2, :]).then_inc(y_out_done[r % 2], 16)
                    if not last or r < 2:
                        load_x(BPC * i + r + 2, r)

            with sp.Fori(0, CHUNKS - 2) as i:
                finish_chunk(i, BPC, False)
            finish_chunk(CHUNKS - 2, 2, False)
            finish_chunk(CHUNKS - 1, 0, True)
            for r in range(2):
                sp.wait_ge(y_out_done[r], 16 * B // 2)

        @block.gpsimd
        def _(pool):
            nc.gpsimd.iota(part_i[:, :], pattern=[[0, 1]], base=0, channel_multiplier=1).then_inc(consts, 1)
            nc.gpsimd.memset(ident32[:, :], 0.0).then_inc(idents, 1)
            nc.gpsimd.memset(ident16[:, :], 0.0).then_inc(idents, 1)
            pool.wait_ge(idents, 2)
            for ident in (ident32, ident16):
                nc.gpsimd.affine_select(out=ident[:, :], in_=ident[:, :], compare_op=ALU.not_equal, fill=1.0,
                                        base=0, pattern=[[-1, P]], channel_multiplier=1).then_inc(idents, 1)

            def over_partitions(which):
                pool.wait_ge(part_max, which + 1)
                nc.gpsimd.partition_all_reduce(am[which], pm[which], P, RMAX).then_inc(all_max, 1)

            for which in (WG, COND, WU, WD, GATE):
                over_partitions(which)

            def codes(i):
                first = isinstance(i, int) and i == 0
                for u in range(steps_of(i)):
                    n, s, turn = gate_step(i, u)
                    loaded, stored = held(pool, 16 * turn + 16), held(pool, 16 * turn)
                    read = held(pool, n - GSLOTS + 1)
                    pool.wait_ge(scale_ready, R_GATE)
                    pool.wait_ge(gate_in[s], loaded)
                    if not first or u >= GSLOTS:
                        pool.wait_ge(gcode_out[s], stored)
                        pool.wait_ge(step_done, read)
                    nc.gpsimd.tensor_scalar(code_ring[:, s, :], gate_ring[:, s, :], k_g, 0.0,
                                            ALU.mult, ALU.add).then_inc(code_made, 1)
                    if u == pool_step(i) + 2:
                        sigmoid_code(n - 2)

            def sigmoid_code(n):
                made, used = held(pool, n + 1), held(pool, n - 1)
                pool.wait_ge(scale_ready, R_GATE)
                pool.wait_ge(sig_made, made)
                pool.wait_ge(step_done, used)
                nc.gpsimd.tensor_scalar(sigq[:, 1, :], sig[:, 1, :], 65536.0, 65535.0,
                                        ALU.mult, ALU.min).then_inc(sigq_pool, 1)

            pool.wait_ge(scale_ready, R_GATE)
            codes(0)
            with pool.Fori(1, HALF) as i:
                codes(i)
            over_partitions(ACTV)

            with pool.Fori(0, PIECES // CSLOTS) as turn:
                for s in range(CSLOTS):
                    loaded, used = held(pool, 16 * turn + 16), held(pool, PIECES + CSLOTS * turn + s - 1)
                    made = held(pool, PIECES + CSLOTS * turn + s + 1)
                    if s < CSLOTS - 1:
                        pool.wait_ge(scale_ready, R_ACT)
                        pool.wait_ge(gcode_in[s], loaded)
                        pool.wait_ge(step_done, used)
                        nc.gpsimd.tensor_scalar(pcode[:, s % 2, :], code_ring[:, s, :], k_p, 0.0,
                                                ALU.mult, ALU.add).then_inc(pcode_pool, 1)
                    pool.wait_ge(scale_ready, R_ACT)
                    pool.wait_ge(sig_made, made)
                    nc.gpsimd.tensor_scalar(sig_int[:, s % 2, :], sig[:, s % 2, :], 65536.0, 0.0,
                                            ALU.mult, ALU.add).then_inc(sig_scaled, 1)
            over_partitions(UP)

            over_partitions(PROD)

        @block.scalar
        def _(act):
            act.dma_start(cat_row[0:CATS, :], cats.rearrange("(a n) -> a n", a=1).to_broadcast([CATS, B]))\
                .then_inc(bias_in, 16)
            act.dma_start(bias_rows[0:CATS, :], cond_b).then_inc(bias_in, 16)

            def copy_xt(i, r, first):
                b = BPC * i + r
                act.wait_ge(x_turned, b + 1)
                if not first or r >= 2:
                    act.wait_ge(cond_done, b - 1)
                nc.scalar.activation(xt[:, r % 2, :, :], psum[4 + r % 2][:, :].rearrange("p (k s) -> p k s", k=KH),
                                     ACT.Copy).then_inc(x_copied, 1)

            def high_part(w, it, j, first):
                n = WSLICES * w + SLICES * it + j
                act.wait_ge(w_stepped, n + 1)
                if not first:
                    act.wait_ge(w_turned, n - SLICES + 1)
                nc.scalar.activation(wparts[:, j, 0, :], ws[:, j, :], ACT.Copy, scale=w_mul[w])\
                    .then_inc(w_high, 1)

            def copy_wt(w, it, j):
                n = WSLICES * w + SLICES * it + j
                act.wait_ge(w_turned, n + 1)
                if w < 2:
                    dst = (wt_gate, wt_up)[w][:, :, :, bass.ds((SLICES * it + j) * P, P)]
                else:
                    dst = wt_down[:, :, 4 * j:4 * j + 4, bass.ds(it * P, P)]
                nc.scalar.activation(dst, wt_bank[:, :, :, :], ACT.Copy).then_inc(wt_ready, 1)

            def cond_chunk(i, first, weights, first_slice=False):
                for r in range(BPC):
                    copy_xt(i, r, first)
                    if weights and r < SLICES:
                        high_part(0, i - 4, r, first_slice)
                    if weights and r >= 2:
                        copy_wt(0, i - 4, r - 2)
                if weights:
                    copy_wt(0, i - 4, SLICES - 1)

            cond_chunk(0, True, False)
            with act.Fori(1, 4) as i:
                cond_chunk(i, False, False)
            act.wait_ge(wscale_ready, 1)
            cond_chunk(4, False, True, True)
            with act.Fori(5, CHUNKS) as i:
                cond_chunk(i, False, True)

            def copy_tile(i, n, first, dram, side):
                q, t = n // PIECE_TILES, NT * i + n
                done = 16 * (Q // 2) * i + 16 * (q // 2)
                if n % PIECE_TILES == 0 and (not first or q >= 2):
                    act.wait_ge(stage_out[q % 2], done)
                    act.wait_ge(piece_maxed, Q * i + q - 1)
                act.wait_ge(tile_done, t + 1)
                nc.scalar.activation(stage[:, q % 2, n % PIECE_TILES, :], psum[n % BANKS][:, :], ACT.Copy)\
                    .then_inc(tile_copied, 1)
                if n % PIECE_TILES == PIECE_TILES - 1:
                    act.wait_ge(tile_copied, t + 1)
                    act.dma_start(piece_rows(dram, Q * i + q - side * PIECES),
                                  stage[:, q % 2, :, :].rearrange("p t c -> p (t c)")).then_inc(stage_out[q % 2], 16)

            def gate_chunk(i, first, w, late):
                it = i if w == 1 else i - 4
                for n in range(NT):
                    copy_tile(i, n, first, gate_dram, 0)
                    if late:
                        if n == 7:
                            act.wait_ge(wscale_ready, w + 1)
                        if 7 <= n < 7 + SLICES:
                            high_part(w, it, n - 7, False)
                        if n >= 10:
                            copy_wt(w, it, n - 10)
                    else:
                        if n % 4 == 1:
                            high_part(w, it, n // 4, False)
                        if n % 4 == 3:
                            copy_wt(w, it, n // 4)
                if late:
                    copy_wt(w, it, SLICES - 1)

            gate_chunk(0, True, 1, True)
            with act.Fori(1, 4) as i:
                gate_chunk(i, False, 1, False)
            gate_chunk(4, False, 2, True)
            with act.Fori(5, CHUNKS) as i:
                gate_chunk(i, False, 2, False)

            def sigmoid(i, u):
                n, s, _ = gate_step(i, u)
                act.wait_ge(code_made, n + 1)
                if not (isinstance(i, int) and i == 0 and u < 2):
                    act.wait_ge(step_done, n - 1)
                nc.scalar.activation(sig[:, u % 2, :], code_ring[:, s, :], ACT.Sigmoid, scale=s_g)\
                    .then_inc(sig_made, 1)
                nc.scalar.activation(mag[:, u % 2, :], code_ring[:, s, :], ACT.Abs).then_inc(mag_made, 1)

            def up_chunk(i):
                u, steps = 0, steps_of(i)
                for n in range(NT):
                    copy_tile(CHUNKS + i, n, False, up_dram, 1)
                    if (n % 3 != 1) if steps == FIRST_STEPS else (n % 2 == 0):
                        if isinstance(i, int) and i == 0 and u == 0:
                            act.wait_ge(scale_ready, R_GATE)
                        sigmoid(i, u)
                        u += 1

            up_chunk(0)
            with act.Fori(1, HALF) as i:
                up_chunk(i)

            n = 0
            for c, count in enumerate(ACT_STEPS):
                for t in range(NT):
                    copy_tile(CHUNKS + HALF + c, t, False, up_dram, 1)
                    if t < count:
                        act.wait_ge(gcode_in[n % CSLOTS], 16 * (n // CSLOTS) + 16)
                        act.wait_ge(step_done, PIECES + n - 1)
                        nc.scalar.activation(sig[:, n % 2, :], code_ring[:, n % CSLOTS, :], ACT.Sigmoid, scale=s_g)\
                            .then_inc(sig_made, 1)
                        if n % CSLOTS == CSLOTS - 1:
                            act.wait_ge(scale_ready, R_ACT)
                            nc.scalar.activation(pcode[:, n % 2, :], code_ring[:, n % CSLOTS, :], ACT.Copy, scale=k_p)\
                                .then_inc(pcode_act, 1)
                        n += 1

            def up_magnitude(src, k, piece):
                nc.scalar.activation(umag[:, k % 2, :], src, ACT.Abs, scale=k_u).then_inc(umag_made, 1)
                if k in MAG_SLOT:
                    nc.scalar.activation(pmag[:, MAG_SLOT[k], :], act_piece(piece), ACT.Abs).then_inc(pmag_act, 1)

            def up_magnitudes(turn):
                for v in range(USLOTS):
                    used, loaded = held(act, USLOTS * turn + v + 1), held(act, 16 * turn + 16)
                    act.wait_ge(scale_ready, R_UP)
                    act.wait_ge(up_in[v], loaded)
                    act.wait_ge(max_used, used)
                    up_magnitude(up_slot(v), v, USLOTS * turn + v)

            act.wait_ge(step_done, 2 * PIECES)
            act.wait_ge(scale_ready, R_UP)
            for k in range(2):
                up_magnitude(stage[:, k, :, :].rearrange("p t c -> p (t c)"), k, PIECES - 2 + k)
            with act.Fori(0, (PIECES - 2) // USLOTS) as turn:
                up_magnitudes(turn)

            def up_codes(i, first):
                for q in range(Q):
                    act.wait_ge(up_again_in[q % 2], 32 * i + (16 if q < 2 else 32))
                    if not first or q >= 2:
                        act.wait_ge(prod_used, Q * i + q - 1)
                    nc.scalar.activation(ucode[:, q % 2, :], up_again[:, q % 2, :], ACT.Copy, scale=k_u)\
                        .then_inc(ucode_made, 1)

            act.wait_ge(umag_made, PIECES)
            up_codes(0, True)
            with act.Fori(1, CHUNKS) as i:
                up_codes(i, False)

        @block.tensor
        def _(pe):
            pe.wait_ge(idents, 4)

            def turn_x(i, r, first):
                b = BPC * i + r
                pe.wait_ge(x_in[r], 16 * i + 16)
                if not first or r >= 2:
                    pe.wait_ge(x_copied, b - 1)
                for k in range(KH):
                    mm = nc.tensor.transpose(psum[4 + r % 2][:, k * S:(k + 1) * S],
                                             x_ring[:, r, k * P:(k + 1) * P], ident32[:, :])
                mm.then_inc(x_turned, 1)

            def cond_matmul(i, r, first):
                b = BPC * i + r
                pe.wait_ge(x_copied, b + 1)
                pe.wait_ge(w_in[r], 16 * i + 16)
                if not first:
                    pe.wait_ge(cond_copied, b - BPC + 1)
                for m in range(KH):
                    for k in range(KH):
                        mm = nc.tensor.matmul(psum[r][:, m * S:(m + 1) * S], w_ring[:, r, k, m * P:(m + 1) * P],
                                              xt[:, r % 2, k, :], start=(k == 0), stop=(k == KH - 1))
                mm.then_inc(cond_done, 1)

            def turn_w(w, it, j, first):
                n = WSLICES * w + SLICES * it + j
                pe.wait_ge(w_low, n + 1)
                if not first:
                    pe.wait_ge(wt_ready, n)
                for h in range(2):
                    for k in range(4):
                        mm = nc.tensor.transpose(wt_bank[:, h, k, :], wparts[:, j, h, k * P:(k + 1) * P], ident16[:, :])
                mm.then_inc(w_turned, 1)

            def cond_chunk(i, first, last, weights):
                for r in range(BPC):
                    if r < BPC - 1:
                        turn_x(i, r + 1, first)
                    elif not last:
                        turn_x(i + 1, 0, False)
                    cond_matmul(i, r, first)
                    if weights and r >= 1:
                        turn_w(0, i - 4, r - 1, isinstance(i, int) and i == 4 and r == 1)

            turn_x(0, 0, True)
            pe.wait_ge(onehot_made, 1)
            for m in range(KH):
                mm = nc.tensor.matmul(bias_bank[:, m * B:(m + 1) * B], bias_rows[0:CATS, m * P:(m + 1) * P],
                                      onehot[0:CATS, :], start=True, stop=True)
            mm.then_inc(bias_summed, 1)
            cond_chunk(0, True, False, False)
            with pe.Fori(1, 4) as i:
                cond_chunk(i, False, False, False)
            cond_chunk(4, False, False, True)
            with pe.Fori(5, CHUNKS - 1) as i:
                cond_chunk(i, False, False, True)
            cond_chunk(CHUNKS - 1, False, True, True)

            def tile_matmul(i, c, n, wt, first):
                t = NT * i + n
                if not first or n >= BANKS:
                    pe.wait_ge(tile_copied, t - BANKS + 1)
                bank = psum[n % BANKS]
                for k in range(KH):
                    if first and n == 0:
                        pe.wait_ge(xq_ready, k + 1)
                    w_hi, w_lo = (wt[:, h, k, n * P:(n + 1) * P] for h in range(2))
                    x_hi, x_lo = (xq_at(c, h)[:, :, k, :].rearrange("p a s -> p (a s)") for h in range(2))
                    nc.tensor.matmul(bank[:, :], w_hi, x_hi, start=(k == 0), stop=False)
                    nc.tensor.matmul(bank[:, :], w_hi, x_lo, start=False, stop=False)
                    mm = nc.tensor.matmul(bank[:, :], w_lo, x_hi, start=False, stop=(k == KH - 1))
                mm.then_inc(tile_done, 1)

            def gate_chunk(i, w, late):
                it = i if w == 1 else i - 4
                first = isinstance(i, int) and i == 0
                if not first:
                    pe.wait_ge(xq_ready, KH + i)
                for n in range(NT):
                    tile_matmul(i, i, n, wt_gate, first)
                    if late and n >= NT - SLICES:
                        turn_w(w, it, n - NT + SLICES, False)
                    if not late and n % 4 == 3:
                        turn_w(w, it, n // 4, False)

            pe.wait_ge(wt_ready, WSLICES)
            gate_chunk(0, 1, True)
            with pe.Fori(1, 4) as i:
                gate_chunk(i, 1, False)
            gate_chunk(4, 2, True)
            with pe.Fori(5, CHUNKS - 1) as i:
                gate_chunk(i, 2, False)
            gate_chunk(CHUNKS - 1, 2, False)
            with pe.Fori(0, CHUNKS - 1) as i:
                for n in range(NT):
                    tile_matmul(CHUNKS + i, i, n, wt_up, False)
            for n in range(NT):
                tile_matmul(2 * CHUNKS - 1, CHUNKS - 1, n, wt_up, False)

            def down_products(h, r, k):
                o_hi, o_lo = (o_parts[h][:, part, k, r * P:(r + 1) * P] for part in range(2))
                nc.tensor.matmul(psum[r][:, :], o_hi, wt_down[:, 0, k, :], start=(k == 0), stop=False)
                nc.tensor.matmul(psum[r][:, :], o_hi, wt_down[:, 1, k, :], start=False, stop=False)
                return nc.tensor.matmul(psum[r][:, :], o_lo, wt_down[:, 0, k, :], start=False, stop=(k == NT - 1))

            def down_chunk(i, h):
                for r in range(BPC):
                    pe.wait_ge(y_made, BPC * i + r - BPC + 1)
                    for k in range(NT):
                        if r == 0 and k % PIECE_TILES == 0:
                            pe.wait_ge(o_ready, Q * i + k // PIECE_TILES + 1)
                        mm = down_products(h, r, k)
                    mm.then_inc(out_done, 1)

            pe.wait_ge(tile_copied, 2 * NT * CHUNKS)
            for k in range(NT):
                if k % PIECE_TILES == 0:
                    pe.wait_ge(o_ready, k // PIECE_TILES + 1)
                for r in range(BPC):
                    mm = down_products(0, r, k)
                    if k == NT - 1:
                        mm.then_inc(out_done, 1)
            down_chunk(1, 1)
            with pe.Fori(1, CHUNKS // 2) as pair:
                for h in range(2):
                    down_chunk(2 * pair + h, h)

        @block.vector
        def _(dve):
            steps = [0]

            def link(ins):
                steps[0] += 1
                ins.then_inc(scalar_step, 1)
                dve.wait_ge(scalar_step, steps[0])

            V = nc.vector

            dve.wait_ge(consts, 1)
            link(V.tensor_copy(part_f[:, :], part_i[:, :]))
            dve.wait_ge(bias_in, 32)
            link(V.tensor_copy(cat_f[0:CATS, :], cat_row[0:CATS, :]))
            V.tensor_scalar(onehot[0:CATS, :], cat_f[0:CATS, :], part_f[0:CATS, 0:1], None,
                            ALU.is_equal).then_inc(onehot_made, 1)

            def weight_steps(w, which):
                link(V.tensor_scalar(wstep[:, w, :], wstep[:, w, :], 1.0 / W_QMAX, TINY, ALU.mult, ALU.max))
                link(V.reciprocal(wrecip[:, w, :], wstep[:, w, :]))
                V.tensor_reduce(pm[which], wstep[:, w, :], AX.X, ALU.max).then_inc(part_max, 1)

            def weight_scale(w, which):
                dve.wait_ge(all_max, which + 1)
                mul_i, div_i, e_i = (a.bitcast(i32) for a in (w_mul[w], w_div[w], tmp[1]))
                link(V.tensor_scalar(tmp[0], am[which], W_QMAX, None, ALU.mult))
                link(V.tensor_scalar(e_i, tmp[0].bitcast(i32), 23, None, ALU.logical_shift_right))
                link(V.tensor_scalar(tmp[2].bitcast(i32), e_i, -1.0, 268.0, ALU.mult, ALU.add))
                link(V.tensor_scalar(mul_i, tmp[2].bitcast(i32), 23, None, ALU.logical_shift_left))
                link(V.tensor_scalar(tmp[2].bitcast(i32), e_i, 14.0, None, ALU.subtract))
                steps[0] += 1
                V.tensor_scalar(div_i, tmp[2].bitcast(i32), 23, None, ALU.logical_shift_left).then_inc(scalar_step, 1)
                dve.wait_ge(scalar_step, steps[0])
                V.tensor_copy(tmp[0], am[which]).then_inc(wscale_ready, 1)

            def blocks(a, w, it, j):
                at = (SLICES * it + j) * TILE_BLOCKS
                return a[:, w, bass.ds(at, TILE_BLOCKS)].unsqueeze(2).to_broadcast([P, TILE_BLOCKS, BLOCK])

            def quantise_slice(w, it, j):
                n = WSLICES * w + SLICES * it + j
                src = wf[:, bass.ds(SLICES * it + j, 1), :].rearrange("p a (g e) -> p (a g) e", e=BLOCK)
                dst = ws[:, j, :].rearrange("p (g e) -> p g e", e=BLOCK)
                V.tensor_tensor(dst, src, blocks(wrecip, w, it, j), ALU.mult).then_inc(w_scaled, 1)
                dve.wait_ge(w_scaled, n + 1)
                V.tensor_scalar(ws[:, j, :], ws[:, j, :], ROUND, ROUND, ALU.add, ALU.subtract).then_inc(w_rounded, 1)
                dve.wait_ge(w_rounded, n + 1)
                V.tensor_tensor(dst, dst, blocks(wstep, w, it, j), ALU.mult).then_inc(w_stepped, 1)

            def low_part(w, it, j):
                n = WSLICES * w + SLICES * it + j
                dve.wait_ge(w_high, n + 1)
                V.scalar_tensor_tensor(out=wparts[:, j, 1, :], in0=ws[:, j, :], scalar=w_mul[w], in1=wparts[:, j, 0, :],
                                       op0=ALU.mult, op1=ALU.subtract).then_inc(w_low, 1)

            def add_bias(i, r):
                b = BPC * i + r
                dve.wait_ge(cond_done, b + 1)
                V.tensor_tensor(cond_chunk_at(i)[:, :, :, r * S:(r + 1) * S].rearrange("p a k s -> p (a k) s"),
                                psum[r][:, :].rearrange("p (k s) -> p k s", k=KH),
                                bias[:, bass.ds(b, 1), :].rearrange("p a k -> p (a k)").unsqueeze(2).to_broadcast([P, KH, S]),
                                ALU.add).then_inc(cond_copied, 1)

            def cond_chunk(i, weights, between=None):
                for r in range(BPC):
                    if weights and r < SLICES:
                        quantise_slice(0, i - 4, r)
                    if weights and r >= 1:
                        low_part(0, i - 4, r - 1)
                    add_bias(i, r)
                    if between:
                        between(r)
                dve.wait_ge(cond_copied, BPC * i + BPC)
                V.tensor_reduce(cond_max[:, bass.ds(i, 1)],
                                cond_chunk_at(i).rearrange("p a k s -> p (a k s)"),
                                AX.X, ALU.max, apply_absolute_value=True)

            dve.wait_ge(bias_summed, 1)
            link(V.tensor_copy(bias[:, :, :], bias_bank[:, 0:KH * B].rearrange("p (k b) -> p b k", k=KH)))
            cond_chunk(0, False)

            def gate_blocks(m):
                dve.wait_ge(wgate_in, 16 * m + 16)
                part = WBLOCKS // KH
                V.tensor_reduce(wstep[:, 0, m * part:(m + 1) * part],
                                wf[:, SLICES * m:SLICES * (m + 1), :].rearrange("p n (g e) -> p (n g) e", e=BLOCK),
                                AX.X, ALU.max, apply_absolute_value=True).then_inc(wblocks_maxed, 1)

            def after_chunk_3(r):
                if r == 0:
                    gate_blocks(3)
                if r == 1:
                    dve.wait_ge(wblocks_maxed, KH)
                    weight_steps(0, WG)
                if r == 3:
                    weight_scale(0, WG)

            cond_chunk(1, False, lambda r: gate_blocks(0) if r == 3 else None)
            cond_chunk(2, False, lambda r: gate_blocks(r // 2 + 1) if r % 2 == 1 else None)
            cond_chunk(3, False, after_chunk_3)
            with dve.Fori(4, CHUNKS - 1) as i:
                cond_chunk(i, True)

            def last_max(r):
                if r >= BPC - 2:
                    dve.wait_ge(cond_copied, B - BPC + r + 1)
                    old = (BPC - 1) * S
                    cols = slice(0, old) if r == BPC - 2 else slice(old, CHUNK)
                    at = CHUNKS - 1 if r == BPC - 2 else CHUNKS
                    link(V.tensor_reduce(cond_max[:, at:at + 1], cond_last[:, 0, :, cols], AX.XY, ALU.max,
                                         apply_absolute_value=True))

            for r in range(BPC):
                if r < SLICES:
                    quantise_slice(0, CHUNKS - 5, r)
                if r >= 1:
                    low_part(0, CHUNKS - 5, r - 1)
                add_bias(CHUNKS - 1, r)
                last_max(r)
            V.tensor_reduce(pm[COND], cond_max[:, :], AX.X, ALU.max).then_inc(part_max, 1)

            dve.wait_ge(all_max, COND + 1)
            link(V.tensor_scalar(s_x, am[COND], 1.0 / ACT_QMAX, TINY, ALU.mult, ALU.max))
            link(V.reciprocal(k_x, s_x))

            def split_codes(i, k=None):
                ks = slice(0, KH) if k is None else slice(k, k + 1)
                code = xcode[:, ks.start * CHUNK:ks.stop * CHUNK]
                count = KH + i if k is None else k + 1
                high, low = (xq_at(i, h)[:, :, ks, :].rearrange("p a k s -> p (a k s)") for h in range(2))
                V.tensor_scalar(high, code, ROUND32, ROUND32, ALU.add, ALU.subtract).then_inc(xhigh_made, 1)
                dve.wait_ge(xhigh_made, count)
                V.tensor_tensor(low, code, high, ALU.subtract).then_inc(xq_ready, 1)
                dve.wait_ge(xq_ready, count)

            def x_codes(i):
                whole = cond_chunk_at(i).rearrange("p a k s -> p (a k s)")
                V.tensor_scalar(xcode[:, :], whole, k_x, None, ALU.mult).then_inc(xcode_made, 1)
                dve.wait_ge(xcode_made, i + 1)
                split_codes(i)

            def piece_max(i, q, side):
                dve.wait_ge(tile_copied, NT * (CHUNKS * side + i) + PIECE_TILES * (q + 1))
                V.tensor_reduce(tile_max[:, side, bass.ds(Q * i + q, 1)], stage[:, q % 2, :, :].rearrange("p t c -> p (t c)"),
                                AX.X, ALU.max, apply_absolute_value=True).then_inc(piece_maxed, 1)

            def last_piece_max(side):
                for n, (a, b) in enumerate(((0, PIECE_TILES - 1), (PIECE_TILES - 1, PIECE_TILES))):
                    dve.wait_ge(tile_copied, NT * CHUNKS * (side + 1) - PIECE_TILES + b)
                    V.tensor_reduce(tile_max[:, side, PIECES - 1 + n:PIECES + n],
                                    stage[:, 1, a:b, :].rearrange("p t c -> p (t c)"),
                                    AX.X, ALU.max, apply_absolute_value=True)\
                        .then_inc(piece_maxed if n else part_maxed, 1)

            def down_blocks(i):
                dve.wait_ge(wdown_tile_in, 16 * i + 16)
                V.tensor_reduce(wstep[:, 2, bass.ds(i * (WBLOCKS // KH), WBLOCKS // KH)],
                                wd_tile[:, :].rearrange("p (g e) -> p g e", e=BLOCK),
                                AX.X, ALU.max, apply_absolute_value=True).then_inc(wdown_maxed, 1)

            def gate_chunk(i, w):
                it = i if w == 1 else i - 4
                last = isinstance(i, int) and i == CHUNKS - 1
                if not last:
                    x_codes(i + 1)
                for q in range(Q):
                    if q < SLICES:
                        quantise_slice(w, it, q)
                        low_part(w, it, q)
                    if last and q == Q - 1:
                        last_piece_max(0)
                    else:
                        piece_max(i, q, 0)
                if w == 1:
                    down_blocks(i)

            def late_chunk(i, w, which):
                piece_max(i, 0, 0)
                weight_steps(w, which)
                weight_scale(w, which)
                if w == 2:
                    dve.wait_ge(wdown_in[KH - 1], 16)
                quantise_slice(w, 0, 0)
                piece_max(i, 1, 0)
                quantise_slice(w, 0, 1)
                quantise_slice(w, 0, 2)
                low_part(w, 0, 0)
                piece_max(i, 2, 0)
                low_part(w, 0, 1)
                low_part(w, 0, 2)
                piece_max(i, 3, 0)
                if w == 1:
                    down_blocks(i)

            V.tensor_scalar(xcode[:, :], cond_head[:, 0, :, :].rearrange("p k s -> p (k s)"), k_x, None, ALU.mult)\
                .then_inc(xcode_made, 1)
            dve.wait_ge(xcode_made, 1)
            for k in range(KH):
                split_codes(0, k)
            V.tensor_copy(tmp[0], s_x).then_inc(wdown_maxed, 1)
            x_codes(1)
            dve.wait_ge(wup_in, 16)
            link(V.tensor_reduce(wstep[:, 1, :], wf[:, :, :].rearrange("p n (g e) -> p (n g) e", e=BLOCK),
                                 AX.X, ALU.max, apply_absolute_value=True))
            late_chunk(0, 1, WU)
            with dve.Fori(1, 4) as i:
                gate_chunk(i, 1)
            x_codes(5)
            dve.wait_ge(wdown_maxed, KH + 1)
            for m in range(KH):
                dve.wait_ge(wdown_in[m], 16)
            late_chunk(4, 2, WD)
            with dve.Fori(5, CHUNKS - 2) as i:
                gate_chunk(i, 2)
            gate_chunk(CHUNKS - 2, 2)
            gate_chunk(CHUNKS - 1, 2)

            def step_from_max(which, values, unit, step, factor):
                V.tensor_reduce(pm[which], values, AX.X, ALU.max).then_inc(part_max, 1)
                dve.wait_ge(all_max, which + 1)
                link(V.tensor_scalar(tmp[0], am[which], unit, 1.0 / ACT_QMAX, ALU.mult, ALU.mult))
                link(V.tensor_scalar(step, tmp[0], TINY, None, ALU.max))
                link(V.reciprocal(tmp[1], step))
                V.tensor_scalar(factor, tmp[1], unit, None, ALU.mult).then_inc(scale_ready, 1)

            dve.wait_ge(part_maxed, 1)
            dve.wait_ge(piece_maxed, PIECES)
            link(V.tensor_scalar(tmp[2], s_x, w_div[0], None, ALU.mult))
            steps[0] += 1
            V.tensor_copy(tmp[0], tmp[2]).then_inc(scalar_step, 1)
            dve.wait_ge(scalar_step, steps[0])
            V.tensor_copy(tmp[1], s_x).then_inc(scale_ready, 1)
            step_from_max(GATE, tile_max[:, 0, :], tmp[2], s_g, k_g)

            def magnitude(dst, src, negative, done, count):
                V.tensor_scalar(negative, src, -1.0, None, ALU.mult).then_inc(neg_made, 1)
                dve.wait_ge(neg_made, count + 1)
                V.tensor_tensor(dst, src, negative, ALU.max).then_inc(done, 1)

            def max_step(i, u):
                first, at = isinstance(i, int) and i == 0, pool_step(i)
                n, own = gate_step(i, u)[0], u - (u > at)
                if not first:
                    own = (LOOP_STEPS - 1) * i + own + FIRST_STEPS - LOOP_STEPS
                done, made, own = held(dve, n), held(dve, n + 1), held(dve, own + 1)
                turn = held(dve, i + 1)
                if u != at:
                    dve.wait_ge(sig_made, made)
                    V.tensor_scalar(sigq[:, u % 2, :], sig[:, u % 2, :], 65536.0, 65535.0, ALU.mult, ALU.min)\
                        .then_inc(sigq_made, 1)
                dve.wait_ge(scale_ready, R_GATE)
                dve.wait_ge(mag_made, made)
                if u == at:
                    dve.wait_ge(sigq_pool, turn)
                else:
                    dve.wait_ge(sigq_made, own)
                if not (first and u == 0):
                    dve.wait_ge(step_done, done)
                V.tensor_tensor_reduce(junk[:, :], mag[:, u % 2, :], sigq[:, u % 2, :], 1.0, 0.0, ALU.mult, ALU.max,
                                       p_max[:, 0, u:u + 1]).then_inc(step_done, 1)

            def act_step(n):
                used = -(-(3 * K * (n + 1) - 24 * K) // (8 * K))
                if used > 0:
                    dve.wait_ge(tile_done, NT * (CHUNKS + min(used, CHUNKS - 1)))
                if n % CSLOTS == CSLOTS - 1:
                    dve.wait_ge(pcode_act, n // CSLOTS + 1)
                else:
                    dve.wait_ge(pcode_pool, n - n // CSLOTS + 1)
                dve.wait_ge(sig_scaled, n + 1)
                V.scalar_tensor_tensor(out=act_piece(n), in0=sig_int[:, n % 2, :], scalar=65535.0,
                                       in1=pcode[:, n % 2, :], op0=ALU.min, op1=ALU.mult).then_inc(step_done, 1)

            link(V.memset(p_max[:, 1, :], 0.0))

            def up_chunk_max(i):
                u = 0
                for q, count in enumerate((2, 2, 2, 2) if steps_of(i) == FIRST_STEPS else (1, 2, 1, 2)):
                    for _ in range(count):
                        max_step(i, u)
                        u += 1
                    piece_max(i, q, 1)
                dve.wait_ge(step_done, gate_step(i, u)[0])
                V.tensor_tensor(p_max[:, 1, :], p_max[:, 1, :], p_max[:, 0, :], ALU.max).then_inc(p_merged, 1)
                dve.wait_ge(p_merged, i + 1)

            up_chunk_max(0)
            with dve.Fori(1, HALF) as i:
                up_chunk_max(i)
            link(V.tensor_scalar(c_p, s_g, 1.0 / 65536.0, None, ALU.mult))
            step_from_max(ACTV, p_max[:, 1, :], c_p, s_p, k_p)
            dve.wait_ge(scale_ready, R_ACT)
            n = 0
            for c, count in enumerate(ACT_STEPS):
                last = c == len(ACT_STEPS) - 1
                for q in range(Q):
                    for _ in range((4, 3, 3, 0)[q] if last else (3, 3, 3, 2)[q]):
                        act_step(n)
                        n += 1
                    if last and q == Q - 1:
                        dve.wait_ge(step_done, 2 * PIECES)
                        magnitude(pmag[:, 0, :], act_piece(PIECES - 2), pneg[:, :], pmag_made, 0)
                        last_piece_max(1)
                    else:
                        piece_max(HALF + c, q, 1)
            assert n == PIECES
            dve.wait_ge(part_maxed, 2)
            dve.wait_ge(piece_maxed, 2 * PIECES)
            link(V.tensor_scalar(tmp[2], s_x, w_div[1], None, ALU.mult))
            step_from_max(UP, tile_max[:, 1, :], tmp[2], s_u, k_u)

            def product_max(v, at, done, umag_count, pmag_sem, pmag_count, first):
                dve.wait_ge(scale_ready, R_UP)
                dve.wait_ge(pmag_sem, pmag_count)
                dve.wait_ge(umag_made, umag_count)
                if not first:
                    dve.wait_ge(max_used, done)
                V.tensor_tensor_reduce(pjunk[:, v % 2, :], pmag[:, at, :], umag[:, v % 2, :], 1.0, 0.0,
                                       ALU.mult, ALU.max, o_max[:, 0, v:v + 1]).then_inc(max_used, 1)

            def merge(count, turn):
                dve.wait_ge(max_used, count)
                V.tensor_tensor(o_max[:, 1, :], o_max[:, 1, :], o_max[:, 0, :], ALU.max).then_inc(o_merged, 1)
                dve.wait_ge(o_merged, turn)

            link(V.memset(o_max[:, :, :], 0.0))
            product_max(0, 0, None, 1, pmag_made, 1, True)
            product_max(1, 1, None, 2, pmag_act, 1, True)
            merge(2, 1)
            with dve.Fori(0, (PIECES - 2) // USLOTS) as turn:
                for v in range(USLOTS):
                    k = USLOTS * turn + v + 2
                    done, umag_count = held(dve, k - 1), held(dve, k + 1)
                    if v in MAG_SLOT:
                        at, made, count = MAG_SLOT[v], pmag_act, len(MAG_SLOT) * turn + list(MAG_SLOT).index(v) + 2
                    else:
                        at, made, count = 0, pmag_made, 2 * turn + v // 2 + 2
                        magnitude(pmag[:, 0, :], act_piece(k - 2), pneg[:, :], pmag_made,
                                  2 * turn + v // 2 + 1)
                    product_max(v, at, done, umag_count, made, held(dve, count), False)
                merge(USLOTS * turn + USLOTS + 2, turn + 2)
            link(V.tensor_scalar(c_o, s_p, s_u, None, ALU.mult))
            step_from_max(PROD, o_max[:, 1, :], c_o, s_o, k_o)
            dve.wait_ge(scale_ready, R_PROD)
            link(V.tensor_scalar(k_y, s_o, w_div[2], None, ALU.mult))

            def product_codes(i, q, h, first):
                n = Q * i + q
                high, low = (o_parts[h][:, part, PIECE_TILES * q:PIECE_TILES * (q + 1), :]
                             .rearrange("p t c -> p (t c)") for part in range(2))
                dve.wait_ge(ucode_made, n + 1)
                V.scalar_tensor_tensor(out=ocode[:, q % 2, :], in0=act_piece(n), scalar=k_o, in1=ucode[:, q % 2, :],
                                       op0=ALU.mult, op1=ALU.mult).then_inc(prod_used, 1)
                dve.wait_ge(prod_used, n + 1)
                if not first and q == 0:
                    dve.wait_ge(out_done, BPC * (i - 1))
                V.tensor_scalar(high, ocode[:, q % 2, :], ROUND32, ROUND32, ALU.add, ALU.subtract)\
                    .then_inc(ohigh_made, 1)
                dve.wait_ge(ohigh_made, n + 1)
                V.tensor_tensor(low, ocode[:, q % 2, :], high, ALU.subtract).then_inc(o_ready, 1)

            def finish_tile(i, r, first):
                dve.wait_ge(out_done, BPC * i + r + 1)
                dve.wait_ge(xres_in[r % 2], 32 * i + (16 if r < 2 else 32))
                if not first or r >= 2:
                    dve.wait_ge(y_out_done[r % 2], 32 * i + (0 if r < 2 else 16))
                V.scalar_tensor_tensor(out=y_out[:, r % 2, :], in0=psum[r][:, :], scalar=k_y, in1=x_res[:, r % 2, :],
                                       op0=ALU.mult, op1=ALU.add).then_inc(y_made, 1)

            for q in range(Q):
                product_codes(0, q, 0, True)
            for q in range(Q):
                product_codes(1, q, 1, True)
                finish_tile(0, q, True)
            with dve.Fori(1, CHUNKS // 2) as pair:
                for h in range(2):
                    i = 2 * pair + h
                    for q in range(Q):
                        product_codes(i, q, h, False)
                        finish_tile(i - 1, q, False)
            for r in range(BPC):
                finish_tile(CHUNKS - 1, r, False)


_INS = ['x', 'itok_B_0_63', 'L0_cond_W', 'L0_cond_b', 'L0_ffn_w_gate', 'L0_ffn_w_up', 'L0_ffn_w_down']
_OUTS = [((B, S, H), 'float32')]


def kernel(**inputs):
    import numpy as _np
    import concourse.bacc as _bacc
    from concourse import mybir as _mybir
    from concourse.bass_utils import run_bass_kernel_spmd as _run

    nc = _bacc.Bacc("TRN2", target_bir_lowering=False, num_devices=1)
    arrays, args = {}, []
    for name in _INS:
        a = _np.ascontiguousarray(inputs[name])
        arrays[f"in_{name}_dram"] = a
        args.append(nc.dram_tensor(f"in_{name}_dram", a.shape, _mybir.dt.from_np(a.dtype), kind="ExternalInput").ap())
    for i, (shape, dtype) in enumerate(_OUTS):
        dt = _mybir.dt.from_np(_np.dtype(dtype))
        args.append(nc.dram_tensor(f"out_{i}_dram", shape, dt, kind="ExternalOutput").ap())
    adaln_ffn(nc, *args)
    r = _run(nc, [arrays], core_ids=[0])
    got = tuple(r.results[0][f"out_{i}_dram"] for i in range(len(_OUTS)))
    return got[0]
```

```python
from contextlib import ExitStack

import concourse.bass as bass
from concourse import mybir


B, S, H = 32, 128, 512
CATS = 64
INNER = 1536
BLOCK = 32

P = 128
CHUNK = 512
CHUNKS = B * S // CHUNK
BPC = CHUNK // S
KH = H // P
NT = INNER // P
PIECE_TILES = 3
PIECE = PIECE_TILES * CHUNK
Q = NT // PIECE_TILES
PIECES = Q * CHUNKS
WCOLS = INNER * H // P
WBLOCKS = WCOLS // BLOCK
TILE_BLOCKS = 512 // BLOCK
SLICES = 3
WSLICES = WCOLS // 512
BANKS = 6
FIRST_STEPS, LOOP_STEPS = 8, 6
PASS_CHUNKS = 5
ACT_STEPS = (11, 10, 10)
SIG3_STEPS = 29
KEPT = 3
CODE_SLOT = (2, 0, 1, 3)
GSLOTS = 3
CSLOTS = 4
USLOTS = 6
MAG_SLOT = {1: 1, 3: 2, 4: 3, 5: 4}
MSLOTS = 3

ACT_QMAX = 32767.0
W_QMAX = 7.0
TINY = 1e-12
ROUND = 1.5 * 2.0 ** 23
ROUND32 = ROUND * 32
RMAX = bass.bass_isa.ReduceOp.max


def adaln_ffn(nc, x, cats, cond_w, cond_b, w_gate, w_up, w_down, out):
    f32, f16, i16 = mybir.dt.float32, mybir.dt.float16, mybir.dt.int16
    i32, u16, bf16 = mybir.dt.int32, mybir.dt.uint16, mybir.dt.bfloat16
    ALU, ACT, AX = mybir.AluOpType, mybir.ActivationFunctionType, mybir.AxisListType

    gate_dram = nc.dram_tensor("gate_scratch", (PIECES, P, PIECE), f32, kind="Internal").ap()
    up_dram = nc.dram_tensor("up_scratch", (PIECES, P, PIECE), f32, kind="Internal").ap()
    gcode_dram = nc.dram_tensor("gate_code_scratch", (PIECES, P, PIECE), i16, kind="Internal").ap()

    ctx = ExitStack()
    with ctx:
        arena = ctx.enter_context(nc.sbuf_tensor("arena", [P, 207 * 1024], mybir.dt.uint8))
        base = nc.sbuf_base - 207 * 1024

        def place(name, offset, shape, dt):
            return nc.alloc_sbuf_tensor_at(name, [P] + shape, dt, offset=base + offset)

        K = 1024
        wt_gate = place("wt_gate", 0, [2, KH, INNER], f16)
        gate_ring = place("gate_ring", 0, [GSLOTS, PIECE], f32)
        cond_head = place("cond_head", 24 * K, [CHUNKS - 1, KH, CHUNK], f32)
        xq_head = place("xq_head", 24 * K, [CHUNKS - 1, 2, KH, CHUNK], f16)
        bias_rows = place("bias_rows", 80 * K, [H], f32)
        onehot = place("onehot", 82 * K, [B], f32)
        xcode = place("xcode", 84 * K, [KH * CHUNK], i16)
        wd_tile = place("wd_tile", 88 * K, [INNER], f32)
        mag = place("mag", 80 * K, [2, PIECE], i16)
        junk = place("junk", 86 * K, [PIECE], bf16)
        act_codes = place("act_codes", 0, [PIECES, PIECE], i16)
        wt_up = place("wt_up", 96 * K, [2, KH, INNER], f16)
        wt_down = place("wt_down", 120 * K, [2, NT, H], f16)
        w_ring = place("w_ring", 96 * K, [BPC, KH, H], f32)
        x_ring = place("x_ring", 128 * K, [BPC, H], f32)
        xt = place("xt", 136 * K, [2, KH, S], f32)
        R = 144 * K
        wf = place("wf", R, [WSLICES, 512], f32)
        ws = place("ws", R + 24 * K, [SLICES, 512], f32)
        wparts = place("wparts", R + 30 * K, [SLICES, 2, 512], f16)
        stage = place("stage", R + 36 * K, [2, PIECE_TILES, CHUNK], f32)
        code_ring = place("code_ring", R, [CSLOTS, PIECE], i16)
        sig = place("sig", R + 12 * K, [2, PIECE], f32)
        sigq = place("sigq", R + 24 * K, [2, PIECE], u16)
        sig_int = place("sig_int", R + 12 * K, [2, PIECE], i32)
        pcode = place("pcode", R + 24 * K, [2, PIECE], f32)
        sig_more = place("sig_more", 80 * K, [PIECE], f32)
        sig_more_int = place("sig_more_int", 80 * K, [PIECE], i32)
        sigq_last = place("sigq_last", R + 30 * K, [PIECE], u16)
        cond_last = place("cond_last", R + 48 * K, [1, KH, CHUNK], f32)
        xq_last = place("xq_last", R + 48 * K, [1, 2, KH, CHUNK], f16)
        up_head = place("up_head", 96 * K, [USLOTS - 2, PIECE], f32)
        up_tail = place("up_tail", R + 36 * K, [2, PIECE], f32)
        umag = place("umag", R, [MSLOTS, PIECE], i16)
        pmag = place("pmag", R + 9 * K, [5, PIECE], i16)
        pjunk = place("pjunk", R + 48 * K, [2, PIECE], bf16)
        o_parts = [place("o_parts0", 96 * K, [2, NT, CHUNK], f16), place("o_parts1", R, [2, NT, CHUNK], f16)]
        up_again = place("up_again", R + 24 * K, [2, PIECE], f32)
        ucode = place("ucode", R + 36 * K, [2, PIECE], i16)
        ocode = place("ocode", R + 42 * K, [2, PIECE], i16)
        x_res = place("x_res", R + 48 * K, [2, H], f32)
        y_out = place("y_out", R + 52 * K, [2, H], f32)
        C = R + 56 * K
        wstep = place("wstep", C, [3, WBLOCKS], f32)
        wrecip = place("wrecip", C + 2304, [3, WBLOCKS], f32)
        ident32 = place("ident32", C + 4608, [P], f32)
        ident16 = place("ident16", C + 5120, [P], f16)
        bias = place("bias", C + 5376, [B, KH], f32)
        cat_f = place("cat_f", C + 5888, [B], f32)
        cat_row = place("cat_row", C + 6016, [B], i32)
        part_i = place("part_i", C + 6144, [1], i32)
        part_f = place("part_f", C + 6176, [1], f32)
        cond_max = place("cond_max", C + 6208, [CHUNKS + 1], f32)
        tile_max = place("tile_max", C + 6272, [2, PIECES + 1], f32)
        p_max = place("p_max", C + 6560, [2, FIRST_STEPS], f32)
        o_max = place("o_max", C + 6624, [2, USLOTS], f32)
        NS = 48
        scal = place("scal", C + 6688, [NS], f32)
        cat_id = place("cat_id", C + 6880, [B], i32)
        assert C + 7008 <= 207 * K

        def cond_chunk_at(i):
            last = isinstance(i, int) and i == CHUNKS - 1
            return cond_last[:, 0:1, :, :] if last else cond_head[:, bass.ds(i, 1), :, :]

        def xq_at(i, part):
            last = isinstance(i, int) and i == CHUNKS - 1
            return xq_last[:, 0:1, part, :, :] if last else xq_head[:, bass.ds(i, 1), part, :, :]

        def act_piece(n):
            return act_codes[:, bass.ds(n, 1), :].rearrange("p a n -> p (a n)")

        def up_slot(s):
            return up_head[:, s, :] if s < USLOTS - 2 else up_tail[:, s - USLOTS + 2, :]

        def gate_step(i, u):
            if isinstance(i, int) and i == 0:
                return u, u % GSLOTS, u // GSLOTS
            lead = FIRST_STEPS - LOOP_STEPS
            return LOOP_STEPS * i + lead + u, (lead + u) % GSLOTS, LOOP_STEPS // GSLOTS * i + (lead + u) // GSLOTS

        def act_step_piece(m):
            return PIECES - KEPT + m if m < KEPT else m - KEPT

        def sig_slot(m):
            return m % 3 if m < SIG3_STEPS else (m - SIG3_STEPS) % 2

        def sig_before(m):
            return max((p + 1 for p in range(m) if sig_slot(p) == sig_slot(m)), default=0)

        def sig_of(m, integer=False):
            if sig_slot(m) == 2:
                return (sig_more_int if integer else sig_more)[:, :]
            return (sig_int if integer else sig)[:, sig_slot(m), :]

        def steps_of(i):
            return FIRST_STEPS if isinstance(i, int) and i == 0 else LOOP_STEPS

        names = iter(range(NS))

        def scalar_column():
            n = next(names)
            return scal[:, n:n + 1]

        psum = [ctx.enter_context(nc.psum_tensor(f"bank{n}", [P, CHUNK], f32)) for n in range(6)]
        wt_bank = ctx.enter_context(nc.psum_tensor("wt_bank", [P, 2, KH, P], f16))
        bias_bank = ctx.enter_context(nc.psum_tensor("bias_bank", [P, 512], f32))

        def sem(name):
            return ctx.enter_context(nc.semaphore(name))

        idx_in, bias_in, wgate_in, wup_in = sem("idx_in"), sem("bias_in"), sem("wgate_in"), sem("wup_in")
        w_in = [sem(f"w_in{n}") for n in range(BPC)]
        x_in = [sem(f"x_in{n}") for n in range(BPC)]
        consts, idents = sem("consts"), sem("idents")
        onehot_made, bias_summed = sem("onehot_made"), sem("bias_summed")
        x_turned, x_copied = sem("x_turned"), sem("x_copied")
        cond_done, cond_copied = sem("cond_done"), sem("cond_copied")
        w_scaled, w_rounded, w_stepped = sem("w_scaled"), sem("w_rounded"), sem("w_stepped")
        w_high, w_low, w_turned, wt_ready = sem("w_high"), sem("w_low"), sem("w_turned"), sem("wt_ready")
        wscale_ready = sem("wscale_ready")
        wblocks_maxed = sem("wblocks_maxed")
        wdown_tile_in, wdown_maxed = sem("wdown_tile_in"), sem("wdown_maxed")
        wdown_in = [sem(f"wdown_in{m}") for m in range(KH)]
        xcode_made, xhigh_made, xq_ready = sem("xcode_made"), sem("xhigh_made"), sem("xq_ready")
        tile_done, tile_copied, piece_maxed = sem("tile_done"), sem("tile_copied"), sem("piece_maxed")
        part_maxed = sem("part_maxed")
        stage_out = [sem(f"stage_out{n}") for n in range(2)]
        gate_in = [sem(f"gate_in{n}") for n in range(GSLOTS)]
        gcode_out = [sem(f"gcode_out{n}") for n in range(GSLOTS)]
        gcode_in = [sem(f"gcode_in{n}") for n in range(CSLOTS)]
        code_made, sig_made, sigq_made = sem("code_made"), sem("sig_made"), sem("sigq_made")
        neg_made, mag_made, step_done = sem("neg_made"), sem("mag_made"), sem("step_done")
        sig_scaled, pcode_pool, pcode_act = sem("sig_scaled"), sem("pcode_pool"), sem("pcode_act")
        up_in = [sem(f"up_in{n}") for n in range(USLOTS)]
        umag_made, pmag_made, pmag_act, max_used = sem("umag_made"), sem("pmag_made"), sem("pmag_act"), sem("max_used")
        up_again_in = [sem(f"up_again_in{n}") for n in range(2)]
        ucode_made, prod_used = sem("ucode_made"), sem("prod_used")
        ohigh_made, o_ready = sem("ohigh_made"), sem("o_ready")
        xres_in = [sem(f"xres_in{n}") for n in range(2)]
        y_out_done = [sem(f"y_out_done{n}") for n in range(2)]
        out_done, y_made = sem("out_done"), sem("y_made")
        p_merged, o_merged = sem("p_merged"), sem("o_merged")
        part_max, all_max = sem("part_max"), sem("all_max")
        scalar_step, scale_ready = sem("scalar_step"), sem("scale_ready")

        pm = [scalar_column() for _ in range(8)]
        am = [scalar_column() for _ in range(8)]
        (WG, COND, WU, WD, GATE, ACTV, UP, PROD) = range(8)
        w_mul = [scalar_column() for _ in range(3)]
        w_div = [scalar_column() for _ in range(3)]
        s_x, k_x = scalar_column(), scalar_column()
        s_g, k_g, s_u, k_u = (scalar_column() for _ in range(4))
        c_p, s_p, k_p = (scalar_column() for _ in range(3))
        c_o, s_o, k_o, k_y = (scalar_column() for _ in range(4))
        tmp = [scalar_column() for _ in range(3)]
        R_X, R_GATE, R_ACT, R_UP, R_PROD = 1, 2, 3, 4, 5

        x_flat = x
        wg_view = w_gate.rearrange("(n p) h -> p n h", p=P)
        wu_view = w_up.rearrange("(n p) h -> p n h", p=P)
        wd_view = w_down.rearrange("(m p) i -> p m i", p=P)
        wf_down = wf[:, :, :].rearrange("p (m j) c -> p m (j c)", m=KH)

        def piece_rows(dram, n):
            return dram[bass.ds(n, 1), :, :].rearrange("a p n -> (a p) n")

        def held(eng, value):
            if not isinstance(value, int):
                eng.compute_val(value)
            return value

        block = ctx.enter_context(nc.Block())

        @block.sync
        def _(sp):
            def load_x_batch(i, r, first):
                b = BPC * i + r
                if not first:
                    turned = held(sp, b - BPC + 1)
                    sp.wait_ge(idx_in, 16)
                    sp.wait_ge(x_turned, turned)
                sp.dma_start(x_ring[:, r, :],
                             x_flat[bass.ds(b, 1), :, :].rearrange("a s d -> (a s) d")).then_inc(x_in[r], 16)

            def load_w_batch(i, r, first):
                b = BPC * i + r
                cat = sp.value_load(cat_id[0:1, bass.ds(b, 1)], min_val=0, max_val=CATS - 1)
                sp.wait_ge(idx_in, 16)
                if not first:
                    sp.wait_ge(cond_done, b - BPC + 1)
                sp.dma_start(w_ring[:, r, :, :],
                             cond_w[bass.ds(cat, 1), :, :].rearrange("a (k p) h -> p (a k) h", p=P))\
                    .then_inc(w_in[r], 16)

            sp.dma_start(cat_id[0:1, :], cats.rearrange("(a n) -> a n", a=1)).then_inc(idx_in, 16)
            load_x_batch(0, 0, True)
            sp.wait_ge(idx_in, 16)
            for r in range(BPC):
                load_w_batch(0, r, True)
                if r < BPC - 1:
                    load_x_batch(0, r + 1, True)

            def load_chunk(i, gate_part):
                for r in range(BPC):
                    load_x_batch(i, r, False)
                    load_w_batch(i, r, False)
                    if gate_part is not None and r % 2 == 1:
                        at = SLICES * (gate_part + r // 2)
                        sp.dma_start(wf[:, at:at + SLICES, :], wg_view[:, at:at + SLICES, :]).then_inc(wgate_in, 16)

            load_chunk(1, 0)
            load_chunk(2, 2)
            with sp.Fori(3, CHUNKS) as i:
                load_chunk(i, None)
            sp.wait_ge(w_stepped, WSLICES)
            sp.dma_start(wf[:, :, :], wu_view).then_inc(wup_in, 16)

            with sp.Fori(0, KH) as m:
                sp.wait_ge(idx_in, 16)
                sp.wait_ge(wdown_maxed, m + 1)
                sp.dma_start(wd_tile[:, :], wd_view[:, bass.ds(m, 1), :].rearrange("p a i -> p (a i)"))\
                    .then_inc(wdown_tile_in, 16)
            sp.wait_ge(w_stepped, 2 * WSLICES)
            for m in range(KH):
                sp.dma_start(wf_down[:, m, :], wd_view[:, m, :]).then_inc(wdown_in[m], 16)

            def load_gate(n, s):
                sp.dma_start(gate_ring[:, s, :], piece_rows(gate_dram, n)).then_inc(gate_in[s], 16)

            def gate_codes(i, last):
                for u in range(steps_of(i)):
                    n, s, _ = gate_step(i, u)
                    made = held(sp, n + 1)
                    sp.wait_ge(idx_in, 16)
                    sp.wait_ge(code_made, made)
                    if not last or u < LOOP_STEPS - KEPT:
                        sp.dma_start(piece_rows(gcode_dram, n), code_ring[:, s, :]).then_inc(gcode_out[s], 16)
                    if not last or u < LOOP_STEPS - GSLOTS:
                        load_gate(n + GSLOTS, s)

            sp.wait_ge(stage_out[0], 16 * PIECES // 2)
            sp.wait_ge(stage_out[1], 16 * PIECES // 2)
            sp.wait_ge(tile_done, NT * CHUNKS)
            for s in range(GSLOTS):
                load_gate(s, s)
            gate_codes(0, False)
            with sp.Fori(1, PASS_CHUNKS - 1) as i:
                gate_codes(i, False)
            gate_codes(PASS_CHUNKS - 1, True)

            def load_codes(n, s):
                sp.dma_start(code_ring[:, s, :], piece_rows(gcode_dram, n)).then_inc(gcode_in[s], 16)

            sp.wait_ge(gcode_out[0], 16)
            load_codes(0, CODE_SLOT[KEPT])
            for s in range(GSLOTS):
                sp.wait_ge(gcode_out[s], 16 * len(range(s, PIECES - KEPT, GSLOTS)))
            with sp.Fori(1, PIECES // CSLOTS) as turn:
                for s in range(CSLOTS):
                    used = held(sp, PIECES + CSLOTS * turn + s - CSLOTS + 1)
                    sp.wait_ge(idx_in, 16)
                    sp.wait_ge(step_done, used)
                    load_codes(CSLOTS * turn + s - KEPT, CODE_SLOT[s])

            def load_up(n, s):
                sp.dma_start(up_slot(s), piece_rows(up_dram, n)).then_inc(up_in[s], 16)

            for n in range(2):
                sp.wait_ge(stage_out[n], 16 * (PIECES - 1))
            sp.wait_ge(tile_done, 2 * NT * CHUNKS)
            for s in range(USLOTS - 2):
                load_up(s, s)
            for n in range(2):
                sp.wait_ge(stage_out[n], 16 * PIECES)
            for s in range(USLOTS - 2, USLOTS):
                sp.wait_ge(umag_made, s - USLOTS + 3)
                load_up(s, s)
            with sp.Fori(1, (PIECES - 2) // USLOTS) as turn:
                for s in range(USLOTS):
                    used = held(sp, 2 + USLOTS * turn + s - USLOTS + 1)
                    sp.wait_ge(idx_in, 16)
                    sp.wait_ge(umag_made, used)
                    load_up(USLOTS * turn + s, s)

            def load_again(n, q):
                sp.dma_start(up_again[:, q % 2, :], piece_rows(up_dram, n)).then_inc(up_again_in[q % 2], 16)

            def load_x(b, r):
                sp.dma_start(x_res[:, r % 2, :], x_flat[bass.ds(b, 1), :, :].rearrange("a s d -> (a s) d"))\
                    .then_inc(xres_in[r % 2], 16)

            sp.wait_ge(step_done, 2 * PIECES)
            for q in range(2):
                load_again(q, q)
            sp.wait_ge(max_used, PIECES)
            for q in range(2):
                load_x(q, q)
            for q in range(Q):
                sp.wait_ge(prod_used, q + 1)
                load_again(q + 2, q)

            def finish_chunk(i, pairs_left, last):
                for r in range(BPC):
                    if r < pairs_left:
                        used = held(sp, Q * i + Q + r + 1)
                        sp.wait_ge(idx_in, 16)
                        sp.wait_ge(prod_used, used)
                        load_again(Q * i + Q + r + 2, r)
                    made = held(sp, BPC * i + r + 1)
                    sp.wait_ge(idx_in, 16)
                    sp.wait_ge(y_made, made)
                    sp.dma_start(out[bass.ds(BPC * i + r, 1), :, :].rearrange("a s h -> (a s) h"),
                                 y_out[:, r % 2, :]).then_inc(y_out_done[r % 2], 16)
                    if not last or r < 2:
                        load_x(BPC * i + r + 2, r)

            with sp.Fori(0, CHUNKS - 2) as i:
                finish_chunk(i, BPC, False)
            finish_chunk(CHUNKS - 2, 2, False)
            finish_chunk(CHUNKS - 1, 0, True)
            for r in range(2):
                sp.wait_ge(y_out_done[r], 16 * B // 2)

        @block.gpsimd
        def _(pool):
            nc.gpsimd.iota(part_i[:, :], pattern=[[0, 1]], base=0, channel_multiplier=1).then_inc(consts, 1)
            nc.gpsimd.memset(ident32[:, :], 0.0).then_inc(idents, 1)
            nc.gpsimd.memset(ident16[:, :], 0.0).then_inc(idents, 1)
            pool.wait_ge(idents, 2)
            for ident in (ident32, ident16):
                nc.gpsimd.affine_select(out=ident[:, :], in_=ident[:, :], compare_op=ALU.not_equal, fill=1.0,
                                        base=0, pattern=[[-1, P]], channel_multiplier=1).then_inc(idents, 1)

            def over_partitions(which):
                pool.wait_ge(part_max, which + 1)
                nc.gpsimd.partition_all_reduce(am[which], pm[which], P, RMAX).then_inc(all_max, 1)

            for which in (WG, COND, WU, WD, GATE):
                over_partitions(which)

            def codes(i):
                first = isinstance(i, int) and i == 0
                for u in range(steps_of(i)):
                    n, s, turn = gate_step(i, u)
                    loaded, stored = held(pool, 16 * turn + 16), held(pool, 16 * turn)
                    read = held(pool, n - GSLOTS + 1)
                    pool.wait_ge(scale_ready, R_GATE)
                    pool.wait_ge(gate_in[s], loaded)
                    if not first or u >= GSLOTS:
                        pool.wait_ge(gcode_out[s], stored)
                        pool.wait_ge(step_done, read)
                    nc.gpsimd.tensor_scalar(code_ring[:, s, :], gate_ring[:, s, :], k_g, 0.0,
                                            ALU.mult, ALU.add).then_inc(code_made, 1)

            pool.wait_ge(scale_ready, R_GATE)
            codes(0)
            with pool.Fori(1, PASS_CHUNKS) as i:
                codes(i)
            over_partitions(ACTV)

            for m in range(PIECES):
                slot = CODE_SLOT[m % CSLOTS]
                if m % 2 == 0:
                    pool.wait_ge(scale_ready, R_ACT)
                    if m < KEPT:
                        pool.wait_ge(code_made, PIECES - KEPT + m + 1)
                    else:
                        pool.wait_ge(gcode_in[slot], 16 * (m // CSLOTS))
                    pool.wait_ge(step_done, PIECES + m - 1)
                    nc.gpsimd.tensor_scalar(pcode[:, 0, :], code_ring[:, slot, :], k_p, 0.0,
                                            ALU.mult, ALU.add).then_inc(pcode_pool, 1)
                if m % CSLOTS != 1:
                    pool.wait_ge(sig_made, PIECES + m + 1)
                    nc.gpsimd.tensor_scalar(sig_of(m, True), sig_of(m), 65536.0, 0.0,
                                            ALU.mult, ALU.add).then_inc(sig_scaled, 1)
            over_partitions(UP)

            over_partitions(PROD)

        @block.scalar
        def _(act):
            act.dma_start(cat_row[0:CATS, :], cats.rearrange("(a n) -> a n", a=1).to_broadcast([CATS, B]))\
                .then_inc(bias_in, 16)
            act.dma_start(bias_rows[0:CATS, :], cond_b).then_inc(bias_in, 16)

            def copy_xt(i, r, first):
                b = BPC * i + r
                act.wait_ge(x_turned, b + 1)
                if not first or r >= 2:
                    act.wait_ge(cond_done, b - 1)
                nc.scalar.activation(xt[:, r % 2, :, :], psum[4 + r % 2][:, :].rearrange("p (k s) -> p k s", k=KH),
                                     ACT.Copy).then_inc(x_copied, 1)

            def high_part(w, it, j, first):
                n = WSLICES * w + SLICES * it + j
                act.wait_ge(w_stepped, n + 1)
                if not first:
                    act.wait_ge(w_turned, n - SLICES + 1)
                nc.scalar.activation(wparts[:, j, 0, :], ws[:, j, :], ACT.Copy, scale=w_mul[w])\
                    .then_inc(w_high, 1)

            def copy_wt(w, it, j):
                n = WSLICES * w + SLICES * it + j
                act.wait_ge(w_turned, n + 1)
                if w < 2:
                    dst = (wt_gate, wt_up)[w][:, :, :, bass.ds((SLICES * it + j) * P, P)]
                else:
                    dst = wt_down[:, :, 4 * j:4 * j + 4, bass.ds(it * P, P)]
                nc.scalar.activation(dst, wt_bank[:, :, :, :], ACT.Copy).then_inc(wt_ready, 1)

            def cond_chunk(i, first, weights, first_slice=False):
                for r in range(BPC):
                    copy_xt(i, r, first)
                    if weights and r == 0 and not first_slice:
                        copy_wt(0, i - 5, SLICES - 1)
                    if weights and r >= 1:
                        high_part(0, i - 4, r - 1, first_slice)
                    if weights and r >= 2:
                        copy_wt(0, i - 4, r - 2)

            cond_chunk(0, True, False)
            with act.Fori(1, 4) as i:
                cond_chunk(i, False, False)
            act.wait_ge(wscale_ready, 1)
            cond_chunk(4, False, True, True)
            with act.Fori(5, CHUNKS) as i:
                cond_chunk(i, False, True)
            copy_wt(0, KH - 1, SLICES - 1)

            def copy_tile(i, n, first, dram, side):
                q, t = n // PIECE_TILES, NT * i + n
                done = 16 * (Q // 2) * i + 16 * (q // 2)
                if n % PIECE_TILES == 0 and (not first or q >= 2):
                    act.wait_ge(stage_out[q % 2], done)
                    act.wait_ge(piece_maxed, Q * i + q - 1)
                act.wait_ge(tile_done, t + 1)
                nc.scalar.activation(stage[:, q % 2, n % PIECE_TILES, :], psum[n % BANKS][:, :], ACT.Copy)\
                    .then_inc(tile_copied, 1)
                if n % PIECE_TILES == PIECE_TILES - 1:
                    act.wait_ge(tile_copied, t + 1)
                    act.dma_start(piece_rows(dram, Q * i + q - side * PIECES),
                                  stage[:, q % 2, :, :].rearrange("p t c -> p (t c)")).then_inc(stage_out[q % 2], 16)

            def gate_chunk(i, first, w, late):
                it = i if w == 1 else i - 4
                for n in range(NT):
                    copy_tile(i, n, first, gate_dram, 0)
                    if late:
                        if n == 7:
                            act.wait_ge(wscale_ready, w + 1)
                        if 7 <= n < 7 + SLICES:
                            high_part(w, it, n - 7, False)
                        if n >= NT - SLICES:
                            copy_wt(w, it, n - NT + SLICES)
                    else:
                        if n % 4 == 1:
                            high_part(w, it, n // 4, False)
                        if n % 4 == 3:
                            copy_wt(w, it, n // 4)

            gate_chunk(0, True, 1, True)
            with act.Fori(1, 4) as i:
                gate_chunk(i, False, 1, False)
            gate_chunk(4, False, 2, True)
            with act.Fori(5, CHUNKS) as i:
                gate_chunk(i, False, 2, False)

            def sigmoid(i, u):
                n, s, _ = gate_step(i, u)
                act.wait_ge(code_made, n + 1)
                if not (isinstance(i, int) and i == 0 and u < 2):
                    act.wait_ge(step_done, n - 1)
                nc.scalar.activation(sig[:, u % 2, :], code_ring[:, s, :], ACT.Sigmoid, scale=s_g)\
                    .then_inc(sig_made, 1)
                nc.scalar.activation(mag[:, u % 2, :], code_ring[:, s, :], ACT.Abs).then_inc(mag_made, 1)

            def up_chunk(i):
                u, steps = 0, steps_of(i)
                for n in range(NT):
                    copy_tile(CHUNKS + i, n, False, up_dram, 1)
                    if (n % 3 != 1) if steps == FIRST_STEPS else (n in (0, 2, 3, 5, 6, 8)):
                        if isinstance(i, int) and i == 0 and u == 0:
                            act.wait_ge(scale_ready, R_GATE)
                        sigmoid(i, u)
                        u += 1

            up_chunk(0)
            with act.Fori(1, PASS_CHUNKS) as i:
                up_chunk(i)

            def act_sigmoid(m):
                slot = CODE_SLOT[m % CSLOTS]
                if m < KEPT:
                    act.wait_ge(code_made, PIECES - KEPT + m + 1)
                else:
                    act.wait_ge(gcode_in[slot], 16 * (m // CSLOTS) + (16 if m % CSLOTS == KEPT else 0))
                act.wait_ge(step_done, PIECES + sig_before(m))
                nc.scalar.activation(sig_of(m), code_ring[:, slot, :], ACT.Sigmoid, scale=s_g)\
                    .then_inc(sig_made, 1)
                if m % CSLOTS == CSLOTS - 1:
                    act.wait_ge(scale_ready, R_ACT)
                    act.wait_ge(step_done, PIECES + m - 1)
                    nc.scalar.activation(pcode[:, m % 2, :], code_ring[:, slot, :], ACT.Copy, scale=k_p)\
                        .then_inc(pcode_act, 1)

            act_sigmoid(0)
            m = 1
            for c, count in enumerate(ACT_STEPS):
                for t in range(NT):
                    copy_tile(CHUNKS + PASS_CHUNKS + c, t, False, up_dram, 1)
                    if t < count:
                        act_sigmoid(m)
                        m += 1

            def up_magnitude(src, slot):
                nc.scalar.activation(umag[:, slot, :], src, ACT.Abs, scale=k_u).then_inc(umag_made, 1)

            def act_magnitude(piece, slot):
                nc.scalar.activation(pmag[:, slot, :], act_piece(piece), ACT.Abs).then_inc(pmag_act, 1)

            def magnitudes(turn, first):
                for v in range(USLOTS):
                    used, loaded = held(act, USLOTS * turn + v + 3 - MSLOTS), held(act, 16 * turn + 16)
                    act.wait_ge(scale_ready, R_UP)
                    act.wait_ge(up_in[v], loaded)
                    if not first or v + 3 > MSLOTS:
                        act.wait_ge(max_used, used)
                    up_magnitude(up_slot(v), (v + 2) % MSLOTS)
                    if v in MAG_SLOT:
                        act_magnitude(USLOTS * turn + v, MAG_SLOT[v])

            act.wait_ge(step_done, 2 * PIECES)
            act_magnitude(PIECES - 1, MAG_SLOT[USLOTS - 1])
            act.wait_ge(scale_ready, R_UP)
            for k in range(2):
                up_magnitude(stage[:, k, :, :].rearrange("p t c -> p (t c)"), k)
            magnitudes(0, True)
            with act.Fori(1, (PIECES - 2) // USLOTS) as turn:
                magnitudes(turn, False)

            def up_codes(i, first):
                for q in range(Q):
                    act.wait_ge(up_again_in[q % 2], 32 * i + (16 if q < 2 else 32))
                    if not first or q >= 2:
                        act.wait_ge(prod_used, Q * i + q - 1)
                    nc.scalar.activation(ucode[:, q % 2, :], up_again[:, q % 2, :], ACT.Copy, scale=k_u)\
                        .then_inc(ucode_made, 1)

            act.wait_ge(umag_made, PIECES)
            up_codes(0, True)
            with act.Fori(1, CHUNKS) as i:
                up_codes(i, False)

        @block.tensor
        def _(pe):
            pe.wait_ge(idents, 4)

            def turn_x(i, r, first):
                b = BPC * i + r
                pe.wait_ge(x_in[r], 16 * i + 16)
                if not first or r >= 2:
                    pe.wait_ge(x_copied, b - 1)
                for k in range(KH):
                    mm = nc.tensor.transpose(psum[4 + r % 2][:, k * S:(k + 1) * S],
                                             x_ring[:, r, k * P:(k + 1) * P], ident32[:, :])
                mm.then_inc(x_turned, 1)

            def cond_matmul(i, r, first):
                b = BPC * i + r
                pe.wait_ge(x_copied, b + 1)
                pe.wait_ge(w_in[r], 16 * i + 16)
                if not first:
                    pe.wait_ge(cond_copied, b - BPC + 1)
                for m in range(KH):
                    for k in range(KH):
                        mm = nc.tensor.matmul(psum[r][:, m * S:(m + 1) * S], w_ring[:, r, k, m * P:(m + 1) * P],
                                              xt[:, r % 2, k, :], start=(k == 0), stop=(k == KH - 1))
                mm.then_inc(cond_done, 1)

            def turn_w(w, it, j, first):
                n = WSLICES * w + SLICES * it + j
                pe.wait_ge(w_low, n + 1)
                if not first:
                    pe.wait_ge(wt_ready, n)
                for h in range(2):
                    for k in range(4):
                        mm = nc.tensor.transpose(wt_bank[:, h, k, :], wparts[:, j, h, k * P:(k + 1) * P], ident16[:, :])
                mm.then_inc(w_turned, 1)

            def cond_chunk(i, first, last, weights):
                for r in range(BPC):
                    if r < BPC - 1:
                        turn_x(i, r + 1, first)
                    elif not last:
                        turn_x(i + 1, 0, False)
                    cond_matmul(i, r, first)
                    if weights and r >= 1:
                        turn_w(0, i - 4, r - 1, isinstance(i, int) and i == 4 and r == 1)

            turn_x(0, 0, True)
            pe.wait_ge(onehot_made, 1)
            for m in range(KH):
                mm = nc.tensor.matmul(bias_bank[:, m * B:(m + 1) * B], bias_rows[0:CATS, m * P:(m + 1) * P],
                                      onehot[0:CATS, :], start=True, stop=True)
            mm.then_inc(bias_summed, 1)
            cond_chunk(0, True, False, False)
            with pe.Fori(1, 4) as i:
                cond_chunk(i, False, False, False)
            cond_chunk(4, False, False, True)
            with pe.Fori(5, CHUNKS - 1) as i:
                cond_chunk(i, False, False, True)
            cond_chunk(CHUNKS - 1, False, True, True)

            def tile_matmul(i, c, n, wt, first):
                t = NT * i + n
                if not first or n >= BANKS:
                    pe.wait_ge(tile_copied, t - BANKS + 1)
                bank = psum[n % BANKS]
                for k in range(KH):
                    if first and n == 0:
                        pe.wait_ge(xq_ready, k + 1)
                    w_hi, w_lo = (wt[:, h, k, n * P:(n + 1) * P] for h in range(2))
                    x_hi, x_lo = (xq_at(c, h)[:, :, k, :].rearrange("p a s -> p (a s)") for h in range(2))
                    nc.tensor.matmul(bank[:, :], w_hi, x_hi, start=(k == 0), stop=False)
                    nc.tensor.matmul(bank[:, :], w_hi, x_lo, start=False, stop=False)
                    mm = nc.tensor.matmul(bank[:, :], w_lo, x_hi, start=False, stop=(k == KH - 1))
                mm.then_inc(tile_done, 1)

            def gate_chunk(i, w, late):
                it = i if w == 1 else i - 4
                first = isinstance(i, int) and i == 0
                if not first:
                    pe.wait_ge(xq_ready, KH + i)
                for n in range(NT):
                    tile_matmul(i, i, n, wt_gate, first)
                    if late and n >= NT - SLICES:
                        turn_w(w, it, n - NT + SLICES, False)
                    if not late and n % 4 == 3:
                        turn_w(w, it, n // 4, False)

            pe.wait_ge(wt_ready, WSLICES)
            gate_chunk(0, 1, True)
            with pe.Fori(1, 4) as i:
                gate_chunk(i, 1, False)
            gate_chunk(4, 2, True)
            with pe.Fori(5, CHUNKS - 1) as i:
                gate_chunk(i, 2, False)
            gate_chunk(CHUNKS - 1, 2, False)
            with pe.Fori(0, CHUNKS - 1) as i:
                for n in range(NT):
                    tile_matmul(CHUNKS + i, i, n, wt_up, False)
            for n in range(NT):
                tile_matmul(2 * CHUNKS - 1, CHUNKS - 1, n, wt_up, False)

            def down_products(h, r, k):
                o_hi, o_lo = (o_parts[h][:, part, k, r * P:(r + 1) * P] for part in range(2))
                nc.tensor.matmul(psum[r][:, :], o_hi, wt_down[:, 0, k, :], start=(k == 0), stop=False)
                nc.tensor.matmul(psum[r][:, :], o_hi, wt_down[:, 1, k, :], start=False, stop=False)
                return nc.tensor.matmul(psum[r][:, :], o_lo, wt_down[:, 0, k, :], start=False, stop=(k == NT - 1))

            def down_chunk(i, h):
                for r in range(BPC):
                    pe.wait_ge(y_made, BPC * i + r - BPC + 1)
                    for k in range(NT):
                        if r == 0 and k % PIECE_TILES == 0:
                            pe.wait_ge(o_ready, Q * i + k // PIECE_TILES + 1)
                        mm = down_products(h, r, k)
                    mm.then_inc(out_done, 1)

            pe.wait_ge(tile_copied, 2 * NT * CHUNKS)
            for q in range(Q):
                pe.wait_ge(o_ready, q + 1)
                for r in range(BPC):
                    for k in range(PIECE_TILES * q, PIECE_TILES * (q + 1)):
                        mm = down_products(0, r, k)
                    if q == Q - 1:
                        mm.then_inc(out_done, 1)
            down_chunk(1, 1)
            with pe.Fori(1, CHUNKS // 2) as pair:
                for h in range(2):
                    down_chunk(2 * pair + h, h)

        @block.vector
        def _(dve):
            steps = [0]

            def link(ins):
                steps[0] += 1
                ins.then_inc(scalar_step, 1)
                dve.wait_ge(scalar_step, steps[0])

            V = nc.vector

            dve.wait_ge(consts, 1)
            link(V.tensor_copy(part_f[:, :], part_i[:, :]))
            dve.wait_ge(bias_in, 32)
            link(V.tensor_copy(cat_f[0:CATS, :], cat_row[0:CATS, :]))
            V.tensor_scalar(onehot[0:CATS, :], cat_f[0:CATS, :], part_f[0:CATS, 0:1], None,
                            ALU.is_equal).then_inc(onehot_made, 1)

            def weight_steps(w, which):
                link(V.tensor_scalar(wstep[:, w, :], wstep[:, w, :], 1.0 / W_QMAX, TINY, ALU.mult, ALU.max))
                link(V.reciprocal(wrecip[:, w, :], wstep[:, w, :]))
                V.tensor_reduce(pm[which], wstep[:, w, :], AX.X, ALU.max).then_inc(part_max, 1)

            def weight_scale(w, which):
                dve.wait_ge(all_max, which + 1)
                mul_i, div_i, e_i = (a.bitcast(i32) for a in (w_mul[w], w_div[w], tmp[1]))
                link(V.tensor_scalar(tmp[0], am[which], W_QMAX, None, ALU.mult))
                link(V.tensor_scalar(e_i, tmp[0].bitcast(i32), 23, None, ALU.logical_shift_right))
                link(V.tensor_scalar(tmp[2].bitcast(i32), e_i, -1.0, 268.0, ALU.mult, ALU.add))
                link(V.tensor_scalar(mul_i, tmp[2].bitcast(i32), 23, None, ALU.logical_shift_left))
                link(V.tensor_scalar(tmp[2].bitcast(i32), e_i, 14.0, None, ALU.subtract))
                steps[0] += 1
                V.tensor_scalar(div_i, tmp[2].bitcast(i32), 23, None, ALU.logical_shift_left).then_inc(scalar_step, 1)
                dve.wait_ge(scalar_step, steps[0])
                V.tensor_copy(tmp[0], am[which]).then_inc(wscale_ready, 1)

            def blocks(a, w, it, j):
                at = (SLICES * it + j) * TILE_BLOCKS
                return a[:, w, bass.ds(at, TILE_BLOCKS)].unsqueeze(2).to_broadcast([P, TILE_BLOCKS, BLOCK])

            def quantise_slice(w, it, j):
                n = WSLICES * w + SLICES * it + j
                src = wf[:, bass.ds(SLICES * it + j, 1), :].rearrange("p a (g e) -> p (a g) e", e=BLOCK)
                dst = ws[:, j, :].rearrange("p (g e) -> p g e", e=BLOCK)
                V.tensor_tensor(dst, src, blocks(wrecip, w, it, j), ALU.mult).then_inc(w_scaled, 1)
                dve.wait_ge(w_scaled, n + 1)
                V.tensor_scalar(ws[:, j, :], ws[:, j, :], ROUND, ROUND, ALU.add, ALU.subtract).then_inc(w_rounded, 1)
                dve.wait_ge(w_rounded, n + 1)
                V.tensor_tensor(dst, dst, blocks(wstep, w, it, j), ALU.mult).then_inc(w_stepped, 1)

            def low_part(w, it, j):
                n = WSLICES * w + SLICES * it + j
                dve.wait_ge(w_high, n + 1)
                V.scalar_tensor_tensor(out=wparts[:, j, 1, :], in0=ws[:, j, :], scalar=w_mul[w], in1=wparts[:, j, 0, :],
                                       op0=ALU.mult, op1=ALU.subtract).then_inc(w_low, 1)

            def add_bias(i, r):
                b = BPC * i + r
                dve.wait_ge(cond_done, b + 1)
                V.tensor_tensor(cond_chunk_at(i)[:, :, :, r * S:(r + 1) * S].rearrange("p a k s -> p (a k) s"),
                                psum[r][:, :].rearrange("p (k s) -> p k s", k=KH),
                                bias[:, bass.ds(b, 1), :].rearrange("p a k -> p (a k)").unsqueeze(2).to_broadcast([P, KH, S]),
                                ALU.add).then_inc(cond_copied, 1)

            def cond_chunk(i, weights, between=None):
                for r in range(BPC):
                    if weights and r < SLICES:
                        quantise_slice(0, i - 4, r)
                    if weights and r >= 1:
                        low_part(0, i - 4, r - 1)
                    add_bias(i, r)
                    if between:
                        between(r)
                dve.wait_ge(cond_copied, BPC * i + BPC)
                V.tensor_reduce(cond_max[:, bass.ds(i, 1)],
                                cond_chunk_at(i).rearrange("p a k s -> p (a k s)"),
                                AX.X, ALU.max, apply_absolute_value=True)

            dve.wait_ge(bias_summed, 1)
            link(V.tensor_copy(bias[:, :, :], bias_bank[:, 0:KH * B].rearrange("p (k b) -> p b k", k=KH)))
            cond_chunk(0, False)

            def gate_blocks(m):
                dve.wait_ge(wgate_in, 16 * m + 16)
                part = WBLOCKS // KH
                V.tensor_reduce(wstep[:, 0, m * part:(m + 1) * part],
                                wf[:, SLICES * m:SLICES * (m + 1), :].rearrange("p n (g e) -> p (n g) e", e=BLOCK),
                                AX.X, ALU.max, apply_absolute_value=True).then_inc(wblocks_maxed, 1)

            def after_chunk_3(r):
                if r == 0:
                    gate_blocks(3)
                if r == 1:
                    dve.wait_ge(wblocks_maxed, KH)
                    weight_steps(0, WG)
                if r == 3:
                    weight_scale(0, WG)

            cond_chunk(1, False, lambda r: gate_blocks(0) if r == 3 else None)
            cond_chunk(2, False, lambda r: gate_blocks(r // 2 + 1) if r % 2 == 1 else None)
            cond_chunk(3, False, after_chunk_3)
            with dve.Fori(4, CHUNKS - 1) as i:
                cond_chunk(i, True)

            def last_max(r):
                if r >= BPC - 2:
                    dve.wait_ge(cond_copied, B - BPC + r + 1)
                    old = (BPC - 1) * S
                    cols = slice(0, old) if r == BPC - 2 else slice(old, CHUNK)
                    at = CHUNKS - 1 if r == BPC - 2 else CHUNKS
                    link(V.tensor_reduce(cond_max[:, at:at + 1], cond_last[:, 0, :, cols], AX.XY, ALU.max,
                                         apply_absolute_value=True))

            for r in range(BPC):
                if r < SLICES:
                    quantise_slice(0, CHUNKS - 5, r)
                if r >= 1:
                    low_part(0, CHUNKS - 5, r - 1)
                add_bias(CHUNKS - 1, r)
                last_max(r)
            V.tensor_reduce(pm[COND], cond_max[:, :], AX.X, ALU.max).then_inc(part_max, 1)

            dve.wait_ge(all_max, COND + 1)
            link(V.tensor_scalar(s_x, am[COND], 1.0 / ACT_QMAX, TINY, ALU.mult, ALU.max))
            link(V.reciprocal(k_x, s_x))

            def split_codes(i, k=None):
                ks = slice(0, KH) if k is None else slice(k, k + 1)
                code = xcode[:, ks.start * CHUNK:ks.stop * CHUNK]
                count = KH + i if k is None else k + 1
                high, low = (xq_at(i, h)[:, :, ks, :].rearrange("p a k s -> p (a k s)") for h in range(2))
                V.tensor_scalar(high, code, ROUND32, ROUND32, ALU.add, ALU.subtract).then_inc(xhigh_made, 1)
                dve.wait_ge(xhigh_made, count)
                V.tensor_tensor(low, code, high, ALU.subtract).then_inc(xq_ready, 1)
                dve.wait_ge(xq_ready, count)

            def x_codes(i):
                whole = cond_chunk_at(i).rearrange("p a k s -> p (a k s)")
                V.tensor_scalar(xcode[:, :], whole, k_x, None, ALU.mult).then_inc(xcode_made, 1)
                dve.wait_ge(xcode_made, i + 1)
                split_codes(i)

            def piece_max(i, q, side):
                dve.wait_ge(tile_copied, NT * (CHUNKS * side + i) + PIECE_TILES * (q + 1))
                V.tensor_reduce(tile_max[:, side, bass.ds(Q * i + q, 1)], stage[:, q % 2, :, :].rearrange("p t c -> p (t c)"),
                                AX.X, ALU.max, apply_absolute_value=True).then_inc(piece_maxed, 1)

            def last_piece_max(side):
                for n, (a, b) in enumerate(((0, PIECE_TILES - 1), (PIECE_TILES - 1, PIECE_TILES))):
                    dve.wait_ge(tile_copied, NT * CHUNKS * (side + 1) - PIECE_TILES + b)
                    V.tensor_reduce(tile_max[:, side, PIECES - 1 + n:PIECES + n],
                                    stage[:, 1, a:b, :].rearrange("p t c -> p (t c)"),
                                    AX.X, ALU.max, apply_absolute_value=True)\
                        .then_inc(piece_maxed if n else part_maxed, 1)

            def down_blocks(i):
                dve.wait_ge(wdown_tile_in, 16 * i + 16)
                V.tensor_reduce(wstep[:, 2, bass.ds(i * (WBLOCKS // KH), WBLOCKS // KH)],
                                wd_tile[:, :].rearrange("p (g e) -> p g e", e=BLOCK),
                                AX.X, ALU.max, apply_absolute_value=True).then_inc(wdown_maxed, 1)

            def gate_chunk(i, w):
                it = i if w == 1 else i - 4
                last = isinstance(i, int) and i == CHUNKS - 1
                if not last:
                    x_codes(i + 1)
                for q in range(Q):
                    if q < SLICES:
                        quantise_slice(w, it, q)
                        low_part(w, it, q)
                    if last and q == Q - 1:
                        last_piece_max(0)
                    else:
                        piece_max(i, q, 0)
                if w == 1:
                    down_blocks(i)

            def late_chunk(i, w, which):
                piece_max(i, 0, 0)
                weight_steps(w, which)
                weight_scale(w, which)
                if w == 2:
                    dve.wait_ge(wdown_in[KH - 1], 16)
                quantise_slice(w, 0, 0)
                piece_max(i, 1, 0)
                quantise_slice(w, 0, 1)
                quantise_slice(w, 0, 2)
                low_part(w, 0, 0)
                piece_max(i, 2, 0)
                low_part(w, 0, 1)
                low_part(w, 0, 2)
                piece_max(i, 3, 0)
                if w == 1:
                    down_blocks(i)

            V.tensor_scalar(xcode[:, :], cond_head[:, 0, :, :].rearrange("p k s -> p (k s)"), k_x, None, ALU.mult)\
                .then_inc(xcode_made, 1)
            dve.wait_ge(xcode_made, 1)
            for k in range(KH):
                split_codes(0, k)
            V.tensor_copy(tmp[0], s_x).then_inc(wdown_maxed, 1)
            x_codes(1)
            dve.wait_ge(wup_in, 16)
            link(V.tensor_reduce(wstep[:, 1, :], wf[:, :, :].rearrange("p n (g e) -> p (n g) e", e=BLOCK),
                                 AX.X, ALU.max, apply_absolute_value=True))
            late_chunk(0, 1, WU)
            with dve.Fori(1, 4) as i:
                gate_chunk(i, 1)
            x_codes(5)
            dve.wait_ge(wdown_maxed, KH + 1)
            for m in range(KH):
                dve.wait_ge(wdown_in[m], 16)
            late_chunk(4, 2, WD)
            with dve.Fori(5, CHUNKS - 2) as i:
                gate_chunk(i, 2)
            gate_chunk(CHUNKS - 2, 2)
            gate_chunk(CHUNKS - 1, 2)

            def step_from_max(which, values, unit, step, factor):
                V.tensor_reduce(pm[which], values, AX.X, ALU.max).then_inc(part_max, 1)
                dve.wait_ge(all_max, which + 1)
                link(V.tensor_scalar(tmp[0], am[which], unit, 1.0 / ACT_QMAX, ALU.mult, ALU.mult))
                link(V.tensor_scalar(step, tmp[0], TINY, None, ALU.max))
                link(V.reciprocal(tmp[1], step))
                V.tensor_scalar(factor, tmp[1], unit, None, ALU.mult).then_inc(scale_ready, 1)

            dve.wait_ge(part_maxed, 1)
            dve.wait_ge(piece_maxed, PIECES)
            link(V.tensor_scalar(tmp[2], s_x, w_div[0], None, ALU.mult))
            steps[0] += 1
            V.tensor_copy(tmp[0], tmp[2]).then_inc(scalar_step, 1)
            dve.wait_ge(scalar_step, steps[0])
            V.tensor_copy(tmp[1], s_x).then_inc(scale_ready, 1)
            step_from_max(GATE, tile_max[:, 0, :], tmp[2], s_g, k_g)

            def magnitude(dst, src, count):
                V.tensor_scalar(dst, src, -1.0, None, ALU.mult).then_inc(neg_made, 1)
                dve.wait_ge(neg_made, count + 1)
                V.tensor_tensor(dst, src, dst, ALU.max).then_inc(pmag_made, 1)

            def max_step(i, u):
                n = gate_step(i, u)[0]
                done, made = held(dve, n), held(dve, n + 1)
                dve.wait_ge(sig_made, made)
                V.tensor_scalar(sigq[:, u % 2, :], sig[:, u % 2, :], 65536.0, 65535.0, ALU.mult, ALU.min)\
                    .then_inc(sigq_made, 1)
                dve.wait_ge(scale_ready, R_GATE)
                dve.wait_ge(mag_made, made)
                dve.wait_ge(sigq_made, made)
                if not (isinstance(i, int) and i == 0 and u == 0):
                    dve.wait_ge(step_done, done)
                V.tensor_tensor_reduce(junk[:, :], mag[:, u % 2, :], sigq[:, u % 2, :], 1.0, 0.0, ALU.mult, ALU.max,
                                       p_max[:, 0, u:u + 1]).then_inc(step_done, 1)

            def act_step(m):
                n, slot = act_step_piece(m), CODE_SLOT[m % CSLOTS]
                used = -(-(3 * (n + 1) - 24) // 8)
                if used > 0 and 3 * n < 80:
                    dve.wait_ge(tile_done, NT * (CHUNKS + min(used, CHUNKS - 1)))
                if m == SIG3_STEPS:
                    dve.wait_ge(step_done, PIECES + m)
                if m % CSLOTS == 1:
                    dve.wait_ge(sig_made, PIECES + m + 1)
                    dve.wait_ge(step_done, PIECES + m - 1)
                    V.tensor_scalar(sigq_last[:, :], sig_of(m), 65536.0, 65535.0, ALU.mult, ALU.min)\
                        .then_inc(sigq_made, 1)
                    dve.wait_ge(sigq_made, PIECES + m // CSLOTS + 1)
                    V.scalar_tensor_tensor(out=act_piece(n), in0=code_ring[:, slot, :], scalar=k_p, in1=sigq_last[:, :],
                                           op0=ALU.mult, op1=ALU.mult).then_inc(step_done, 1)
                    return
                if m % CSLOTS == CSLOTS - 1:
                    dve.wait_ge(pcode_act, m // CSLOTS + 1)
                else:
                    dve.wait_ge(pcode_pool, m // 2 + 1)
                dve.wait_ge(sig_scaled, m + 1 - (m + 3) // CSLOTS)
                V.scalar_tensor_tensor(out=act_piece(n), in0=sig_of(m, True), scalar=65535.0,
                                       in1=pcode[:, m % 2, :], op0=ALU.min, op1=ALU.mult).then_inc(step_done, 1)

            link(V.memset(p_max[:, 1, :], 0.0))

            def up_chunk_max(i, last=False):
                u = 0
                for q, count in enumerate((2, 2, 2, 2) if steps_of(i) == FIRST_STEPS else (1, 2, 2, 1)):
                    for _ in range(count):
                        max_step(i, u)
                        u += 1
                    if q == Q - 1:
                        dve.wait_ge(step_done, gate_step(i, u)[0])
                        V.tensor_tensor(p_max[:, 1, :], p_max[:, 1, :], p_max[:, 0, :], ALU.max).then_inc(p_merged, 1)
                        dve.wait_ge(p_merged, i + 1)
                        if last:
                            link(V.tensor_scalar(c_p, s_g, 1.0 / 65536.0, None, ALU.mult))
                            step_from_max(ACTV, p_max[:, 1, :], c_p, s_p, k_p)
                    piece_max(i, q, 1)

            up_chunk_max(0)
            with dve.Fori(1, PASS_CHUNKS - 1) as i:
                up_chunk_max(i)
            up_chunk_max(PASS_CHUNKS - 1, True)
            dve.wait_ge(scale_ready, R_ACT)
            act_step(0)
            m = 1
            for c in range(len(ACT_STEPS)):
                last = c == len(ACT_STEPS) - 1
                for q in range(Q):
                    for _ in range(((3, 3, 3, 2), (3, 3, 3, 1), (4, 3, 2, 1))[c][q]):
                        act_step(m)
                        m += 1
                    if last and q == Q - 1:
                        dve.wait_ge(step_done, 2 * PIECES)
                        magnitude(pmag[:, 0, :], act_piece(PIECES - 2), 0)
                        last_piece_max(1)
                    else:
                        piece_max(PASS_CHUNKS + c, q, 1)
            assert m == PIECES
            dve.wait_ge(part_maxed, 2)
            dve.wait_ge(piece_maxed, 2 * PIECES)
            link(V.tensor_scalar(tmp[2], s_x, w_div[1], None, ALU.mult))
            step_from_max(UP, tile_max[:, 1, :], tmp[2], s_u, k_u)

            def product_max(v, slot, at, done, umag_count, pmag_sem, pmag_count, first):
                dve.wait_ge(scale_ready, R_UP)
                dve.wait_ge(pmag_sem, pmag_count)
                dve.wait_ge(umag_made, umag_count)
                if not first:
                    dve.wait_ge(max_used, done)
                V.tensor_tensor_reduce(pjunk[:, v % 2, :], pmag[:, at, :], umag[:, slot, :], 1.0, 0.0,
                                       ALU.mult, ALU.max, o_max[:, 0, v:v + 1]).then_inc(max_used, 1)

            def merge(count, turn):
                dve.wait_ge(max_used, count)
                V.tensor_tensor(o_max[:, 1, :], o_max[:, 1, :], o_max[:, 0, :], ALU.max).then_inc(o_merged, 1)
                dve.wait_ge(o_merged, turn)

            link(V.memset(o_max[:, :, :], 0.0))
            product_max(0, 0, 0, None, 1, pmag_made, 1, True)
            product_max(1, 1, MAG_SLOT[USLOTS - 1], None, 2, pmag_act, 1, True)
            merge(2, 1)
            with dve.Fori(0, (PIECES - 2) // USLOTS) as turn:
                for v in range(USLOTS):
                    k = USLOTS * turn + v + 2
                    done, umag_count = held(dve, k - 1), held(dve, k + 1)
                    if v in MAG_SLOT:
                        at, made, count = MAG_SLOT[v], pmag_act, len(MAG_SLOT) * turn + list(MAG_SLOT).index(v) + 2
                    else:
                        at, made, count = 0, pmag_made, 2 * turn + v // 2 + 2
                        if v == 2:
                            dve.wait_ge(max_used, k - 1)
                        magnitude(pmag[:, 0, :], act_piece(k - 2), 2 * turn + v // 2 + 1)
                    product_max(v, (v + 2) % MSLOTS, at, done, umag_count, made, held(dve, count), False)
                merge(USLOTS * turn + USLOTS + 2, turn + 2)
            link(V.tensor_scalar(c_o, s_p, s_u, None, ALU.mult))
            step_from_max(PROD, o_max[:, 1, :], c_o, s_o, k_o)
            dve.wait_ge(scale_ready, R_PROD)
            link(V.tensor_scalar(k_y, s_o, w_div[2], None, ALU.mult))

            def product_codes(i, q, h, first):
                n = Q * i + q
                high, low = (o_parts[h][:, part, PIECE_TILES * q:PIECE_TILES * (q + 1), :]
                             .rearrange("p t c -> p (t c)") for part in range(2))
                dve.wait_ge(ucode_made, n + 1)
                V.scalar_tensor_tensor(out=ocode[:, q % 2, :], in0=act_piece(n), scalar=k_o, in1=ucode[:, q % 2, :],
                                       op0=ALU.mult, op1=ALU.mult).then_inc(prod_used, 1)
                dve.wait_ge(prod_used, n + 1)
                if not first and q == 0:
                    dve.wait_ge(out_done, BPC * (i - 1))
                V.tensor_scalar(high, ocode[:, q % 2, :], ROUND32, ROUND32, ALU.add, ALU.subtract)\
                    .then_inc(ohigh_made, 1)
                dve.wait_ge(ohigh_made, n + 1)
                V.tensor_tensor(low, ocode[:, q % 2, :], high, ALU.subtract).then_inc(o_ready, 1)

            def finish_tile(i, r, first):
                dve.wait_ge(out_done, BPC * i + r + 1)
                dve.wait_ge(xres_in[r % 2], 32 * i + (16 if r < 2 else 32))
                if not first or r >= 2:
                    dve.wait_ge(y_out_done[r % 2], 32 * i + (0 if r < 2 else 16))
                V.scalar_tensor_tensor(out=y_out[:, r % 2, :], in0=psum[r][:, :], scalar=k_y, in1=x_res[:, r % 2, :],
                                       op0=ALU.mult, op1=ALU.add).then_inc(y_made, 1)

            for q in range(Q):
                product_codes(0, q, 0, True)
            for q in range(Q):
                if q == Q - 1:
                    finish_tile(0, 0, True)
                product_codes(1, q, 1, True)
            for r in range(1, BPC):
                finish_tile(0, r, True)
            with dve.Fori(1, CHUNKS // 2) as pair:
                for h in range(2):
                    i = 2 * pair + h
                    for q in range(Q):
                        product_codes(i, q, h, False)
                        finish_tile(i - 1, q, False)
            for r in range(BPC):
                finish_tile(CHUNKS - 1, r, False)


_INS = ['x', 'itok_B_0_63', 'L0_cond_W', 'L0_cond_b', 'L0_ffn_w_gate', 'L0_ffn_w_up', 'L0_ffn_w_down']
_OUTS = [((B, S, H), 'float32')]


def kernel(**inputs):
    import numpy as _np
    import concourse.bacc as _bacc
    from concourse import mybir as _mybir
    from concourse.bass_utils import run_bass_kernel_spmd as _run

    nc = _bacc.Bacc("TRN2", target_bir_lowering=False, num_devices=1)
    arrays, args = {}, []
    for name in _INS:
        a = _np.ascontiguousarray(inputs[name])
        arrays[f"in_{name}_dram"] = a
        args.append(nc.dram_tensor(f"in_{name}_dram", a.shape, _mybir.dt.from_np(a.dtype), kind="ExternalInput").ap())
    for i, (shape, dtype) in enumerate(_OUTS):
        dt = _mybir.dt.from_np(_np.dtype(dtype))
        args.append(nc.dram_tensor(f"out_{i}_dram", shape, dt, kind="ExternalOutput").ap())
    adaln_ffn(nc, *args)
    r = _run(nc, [arrays], core_ids=[0])
    got = tuple(r.results[0][f"out_{i}_dram"] for i in range(len(_OUTS)))
    return got[0]
```
